# Optimizing a Trainium2 kernel written in Bass

```python
import numpy as np
import jax
import jax.numpy as jnp

def _softmax(x, axis=-1):
    return jax.nn.softmax(x, axis=axis)

def _gelu(x):
    return jax.nn.gelu(x, approximate=True)

def _silu(x):
    return jax.nn.silu(x)

def _sigmoid(x):
    return jax.nn.sigmoid(x)

def _layernorm(x, axis=-1, eps=1e-05):
    m = jnp.mean(x, axis=axis, keepdims=True)
    v = jnp.var(x, axis=axis, keepdims=True)
    return (x - m) / jnp.sqrt(v + eps)

def _scatter_add(tgt, idx, src, axis=0):
    return tgt.at[idx].add(src)

def _segment_sum(src, seg, n):
    return jax.ops.segment_sum(src, seg, n)
kernel_name = 'mk_xattn_ffn_d2_seqx_r4_a81c22'

def setup_inputs(seed: int=0):
    np.random.seed(seed)
    _w = jnp.asarray

    def _rec_inputs():
        import jax
        import jax.numpy as jnp
        _rk = jax.random.key(seed)
        x = -0.0005146 + 1 * jax.random.normal(jax.random.fold_in(_rk, 1), (4, 1024, 256), jnp.float32)
        _lenS = 1024 - jax.random.randint(jax.random.fold_in(_rk, 7), (4,), 0, max(1, 1024 // 4) + 1, jnp.int32)
        _lenS2 = 154 - jax.random.randint(jax.random.fold_in(_rk, 8), (4,), 0, max(1, 154 // 4) + 1, jnp.int32)
        _ctx_768P = jax.random.normal(jax.random.fold_in(_rk, 11), (4, 16, 192), jnp.float32)
        _ctx_768c = jax.random.dirichlet(jax.random.fold_in(_rk, 511), 0.3 * jnp.ones((16,), jnp.float32), (4, 154))
        _ctx_768t = jnp.einsum('bsk,bkd->bsd', _ctx_768c, _ctx_768P)
        _ctx_768t = _ctx_768t * jax.lax.rsqrt(jnp.mean(jnp.square(_ctx_768t)) + 1e-12) * 0.953939
        ctx_768 = -0.00040386 + 0.999972 * (_ctx_768t + 0.3 * jax.random.normal(jax.random.fold_in(_rk, 611), (4, 154, 192), jnp.float32))
        _validS = jnp.arange(1024)[None, :] < _lenS[:, None]
        _validS2 = jnp.arange(154)[None, :] < _lenS2[:, None]
        _causal = jnp.tril(jnp.ones((1024, 1024), dtype=bool))
        mask_BxS2_bk0 = jnp.logical_not(jnp.broadcast_to(_validS2[:, :], (4, 154)))
        return (x, ctx_768, mask_BxS2_bk0)
    x, ctx_768, mask_BxS2_bk0 = _rec_inputs()

    def _L0_xattn_setup():
        import jax, jax.numpy as jnp
        import numpy as np
        DIM_IN, DIM_LAT, DIM_HEAD = (192, 256, 64)
        INNER = max(DIM_LAT, DIM_IN)
        HEADS = INNER // DIM_HEAD
        SCALE = DIM_HEAD ** (-0.5)
        RMS_EPS = 1e-08
        LN_EPS = 1e-05

        def layernorm(x, g, b):
            mu = jnp.mean(x, axis=-1, keepdims=True)
            var = jnp.mean((x - mu) ** 2, axis=-1, keepdims=True)
            return (x - mu) * jax.lax.rsqrt(var + LN_EPS) * g + b

        def rmsnorm(x, gamma):
            norm = jnp.sqrt(jnp.sum(x * x, axis=-1, keepdims=True)) * x.shape[-1] ** (-0.5)
            return x / jnp.maximum(norm, RMS_EPS) * gamma
        key = jax.random.key(seed)
        ks = jax.random.split(key, 12)
        b, n, m = (4, 1024, 128)
        x = jax.random.normal(ks[0], (b, n, DIM_IN), jnp.float32)
        latents = jax.random.normal(ks[1], (b, m, DIM_LAT), jnp.float32)
        mask = jax.random.randint(ks[2], (b, n), 0, 2).astype(bool)
        s = lambda k, sh, fan: jax.random.normal(k, sh, jnp.float32) * fan ** (-0.5)
        return {'x': x, 'latents': latents, 'mask': mask, 'ln_x_g': jnp.ones((DIM_IN,), jnp.float32), 'ln_x_b': jnp.zeros((DIM_IN,), jnp.float32), 'ln_l_g': jnp.ones((DIM_LAT,), jnp.float32), 'ln_l_b': jnp.zeros((DIM_LAT,), jnp.float32), 'qn_g': jnp.ones((DIM_HEAD,), jnp.float32), 'kn_g': jnp.ones((DIM_HEAD,), jnp.float32), 'Wq': s(ks[3], (INNER, DIM_LAT), DIM_LAT), 'Wkv': s(ks[4], (2 * INNER, DIM_IN), DIM_IN), 'Wlkv': s(ks[5], (2 * INNER, DIM_LAT), DIM_LAT), 'Wo': s(ks[6], (DIM_LAT, INNER), INNER), 'bo': jnp.zeros((DIM_LAT,), jnp.float32)}
    _L0_xattn_all = _L0_xattn_setup()
    _L0_xattn_in = {k: v for k, v in _L0_xattn_all.items() if k in ('ln_x_g', 'ln_x_b', 'ln_l_g', 'ln_l_b', 'qn_g', 'kn_g', 'Wq', 'Wkv', 'Wlkv', 'Wo', 'bo')}
    del _L0_xattn_all

    def _L0_ffn_setup():
        import jax, jax.numpy as jnp
        import numpy as np
        D_MODEL = 256
        FFN_DIM = 512
        NUM_EXPERTS = 8
        NUM_GROUPS = 4
        EXPERTS_PER_GROUP = NUM_EXPERTS // NUM_GROUPS
        TOP_K = 2
        GROUPS_TOP_K = 1
        EPS = 1e-09

        def _topk_normalized(scores, k):
            vals, idx = jax.lax.top_k(scores, k)
            vals = vals / (jnp.sum(vals, axis=-1, keepdims=True) + EPS)
            return (vals, idx)
        key = jax.random.key(seed)
        ks = jax.random.split(key, 6)
        B, S = (2, 256)
        x = jax.random.normal(ks[0], (B, S, D_MODEL), dtype=jnp.float32)
        sd = 0.02
        macro_w = jax.random.normal(ks[1], (D_MODEL, NUM_GROUPS), dtype=jnp.float32) * sd
        micro_w = jax.random.normal(ks[2], (NUM_GROUPS, D_MODEL, EXPERTS_PER_GROUP), dtype=jnp.float32) * sd
        gate_w = jax.random.normal(ks[3], (NUM_EXPERTS, D_MODEL, FFN_DIM), dtype=jnp.float32) * sd
        up_w = jax.random.normal(ks[4], (NUM_EXPERTS, D_MODEL, FFN_DIM), dtype=jnp.float32) * sd
        down_w = jax.random.normal(ks[5], (NUM_EXPERTS, FFN_DIM, D_MODEL), dtype=jnp.float32) * sd
        return {'x': x, 'macro_w': macro_w, 'micro_w': micro_w, 'gate_w': gate_w, 'up_w': up_w, 'down_w': down_w}
    _L0_ffn_all = _L0_ffn_setup()
    _L0_ffn_in = {k: v for k, v in _L0_ffn_all.items() if k in ('macro_w', 'micro_w', 'gate_w', 'up_w', 'down_w')}
    del _L0_ffn_all

    def _L1_xattn_setup():
        import jax, jax.numpy as jnp
        import numpy as np
        B, LQ, LKV = (4, 128, 512)
        DQ, DKV, H = (256, 192, 16)
        HD = DQ // H
        key = jax.random.key(seed)
        ks = jax.random.split(key, 12)
        s_q = 1.0 / np.sqrt(DQ)
        s_kv = 1.0 / np.sqrt(DKV)
        return {'q': jax.random.normal(ks[0], (B, LQ, DQ), jnp.float32), 'kv': jax.random.normal(ks[1], (B, LKV, DKV), jnp.float32), 'Wq': jax.random.normal(ks[2], (DQ, DQ), jnp.float32) * s_q, 'bq': jnp.zeros((DQ,), jnp.float32), 'Wk': jax.random.normal(ks[3], (DKV, DQ), jnp.float32) * s_kv, 'bk': jnp.zeros((DQ,), jnp.float32), 'Wv': jax.random.normal(ks[4], (DKV, DQ), jnp.float32) * s_kv, 'bv': jnp.zeros((DQ,), jnp.float32), 'Wo': jax.random.normal(ks[5], (DQ, DQ), jnp.float32) * s_q, 'bo': jnp.zeros((DQ,), jnp.float32), 'scale': jnp.ones((1,), jnp.float32) * DQ ** (-0.5)}
    _L1_xattn_all = _L1_xattn_setup()
    _L1_xattn_in = {k: v for k, v in _L1_xattn_all.items() if k in ('Wq', 'bq', 'Wk', 'bk', 'Wv', 'bv', 'Wo', 'bo', 'scale')}
    del _L1_xattn_all

    def _L1_ffn_setup():
        import jax, jax.numpy as jnp
        import numpy as np
        DIM = 256
        DEPTH = 2
        HEADS = 8
        DIM_HEAD = 64
        WINDOW = 128
        INNER = HEADS * DIM_HEAD
        HID = int(DIM * 4 * 2 / 3)
        B, N = (2, 2048)
        QK_SCALE = 8.0

        def shift_token(t):
            t1, t2 = jnp.split(t, 2, axis=-1)
            t2 = jnp.pad(t2, ((0, 0), (1, 0), (0, 0)))[:, :-1]
            return jnp.concatenate([t1, t2], axis=-1)

        def l2norm(t):
            return t / jnp.clip(jnp.linalg.norm(t, axis=-1, keepdims=True), 1e-12)

        def rotate_half(x):
            x1, x2 = jnp.split(x, 2, axis=-1)
            return jnp.concatenate([-x2, x1], axis=-1)

        def rotary_xpos(q, k):
            n = q.shape[-2]
            half_idx = jnp.arange(0, DIM_HEAD, 2, dtype=jnp.float32)
            inv_freq = 1.0 / 10000.0 ** (half_idx / DIM_HEAD)
            t = jnp.arange(n, dtype=jnp.float32)
            freqs = t[:, None] * inv_freq[None, :]
            freqs = jnp.concatenate([freqs, freqs], axis=-1)
            base = (half_idx + 0.4 * DIM_HEAD) / (1.4 * DIM_HEAD)
            power = (t - n // 2) / float(WINDOW // 2)
            scale = base[None, :] ** power[:, None]
            scale = jnp.concatenate([scale, scale], axis=-1)
            cos, sin = (jnp.cos(freqs), jnp.sin(freqs))
            q = q * cos * scale + rotate_half(q) * sin * scale
            k = k * cos / scale + rotate_half(k) * sin / scale
            return (q, k)

        def local_attention(q, k, v):
            b, h, n, d = q.shape
            w = n // WINDOW
            bq = q.reshape(b, h, w, WINDOW, d) * QK_SCALE
            bk = k.reshape(b, h, w, WINDOW, d)
            bv = v.reshape(b, h, w, WINDOW, d)

            def look_around(t):
                p = jnp.pad(t, ((0, 0), (0, 0), (1, 0), (0, 0), (0, 0)))
                return jnp.concatenate([p[:, :, :w], p[:, :, 1:]], axis=3)
            bk, bv = (look_around(bk), look_around(bv))
            bt = jnp.arange(n).reshape(w, WINDOW)
            btp = jnp.pad(bt, ((1, 0), (0, 0)), constant_values=-1)
            btk = jnp.concatenate([btp[:w], btp[1:]], axis=1)
            sim = jnp.einsum('bhwid,bhwjd->bhwij', bq, bk)
            i = bt[:, :, None]
            j = btk[:, None, :]
            mask = (i < j) | (i > j + WINDOW) | (j == -1)
            sim = jnp.where(mask, -jnp.finfo(sim.dtype).max, sim)
            attn = jax.nn.softmax(sim, axis=-1)
            out = jnp.einsum('bhwij,bhwjd->bhwid', attn, bv)
            return out.reshape(b, h, n, d)

        def _layer(x, wqkv, qs, ksc, wo, lg, lb, w1, b1, w2, b2):
            b, n, _ = x.shape
            h = shift_token(x)
            qkv = h @ wqkv
            q, k, v = jnp.split(qkv, 3, axis=-1)
            to_heads = lambda t: t.reshape(b, n, HEADS, DIM_HEAD).transpose(0, 2, 1, 3)
            q, k, v = (to_heads(q), to_heads(k), to_heads(v))
            q = l2norm(q) * qs
            k = l2norm(k) * ksc
            q, k = rotary_xpos(q, k)
            o = local_attention(q, k, v)
            o = o.transpose(0, 2, 1, 3).reshape(b, n, INNER)
            x = x + o @ wo
            h = shift_token(x)
            mu = h.mean(-1, keepdims=True)
            var = h.var(-1, keepdims=True)
            h = (h - mu) / jnp.sqrt(var + 1e-05) * lg + lb
            h = h @ w1 + b1
            a, g = jnp.split(h, 2, axis=-1)
            h = a * jax.nn.gelu(g, approximate=False)
            x = x + h @ w2 + b2
            return x
        key = jax.random.key(seed)
        ks = jax.random.split(key, 6)
        return {'x': jax.random.normal(ks[0], (B, N, DIM), jnp.float32), 'wqkv': jax.random.normal(ks[1], (DEPTH, DIM, 3 * INNER), jnp.float32) * 0.02, 'q_scale': jnp.ones((DEPTH, DIM_HEAD), jnp.float32), 'k_scale': jnp.ones((DEPTH, DIM_HEAD), jnp.float32), 'wo': jax.random.normal(ks[2], (DEPTH, INNER, DIM), jnp.float32) * 0.02, 'ln_g': jnp.ones((DEPTH, DIM), jnp.float32), 'ln_b': jnp.zeros((DEPTH, DIM), jnp.float32), 'w1': jax.random.normal(ks[3], (DEPTH, DIM, 2 * HID), jnp.float32) * 0.02, 'b1': jnp.zeros((DEPTH, 2 * HID), jnp.float32), 'w2': jax.random.normal(ks[4], (DEPTH, HID, DIM), jnp.float32) * 0.02, 'b2': jnp.zeros((DEPTH, DIM), jnp.float32)}
    _L1_ffn_all = _L1_ffn_setup()
    _L1_ffn_in = {k: v for k, v in _L1_ffn_all.items() if k in ('wqkv', 'q_scale', 'k_scale', 'wo', 'ln_g', 'ln_b', 'w1', 'b1', 'w2', 'b2')}
    del _L1_ffn_all
    return {'x': x, 'ctx_768': ctx_768, 'mask_BxS2_bk0': mask_BxS2_bk0, 'L0_xattn_ln_x_g': _L0_xattn_in['ln_x_g'], 'L0_xattn_ln_x_b': _L0_xattn_in['ln_x_b'], 'L0_xattn_ln_l_g': _L0_xattn_in['ln_l_g'], 'L0_xattn_ln_l_b': _L0_xattn_in['ln_l_b'], 'L0_xattn_qn_g': _L0_xattn_in['qn_g'], 'L0_xattn_kn_g': _L0_xattn_in['kn_g'], 'L0_xattn_Wq': _L0_xattn_in['Wq'], 'L0_xattn_Wkv': _L0_xattn_in['Wkv'], 'L0_xattn_Wlkv': _L0_xattn_in['Wlkv'], 'L0_xattn_Wo': _L0_xattn_in['Wo'], 'L0_xattn_bo': _L0_xattn_in['bo'], 'L0_ffn_macro_w': _L0_ffn_in['macro_w'], 'L0_ffn_micro_w': _L0_ffn_in['micro_w'], 'L0_ffn_gate_w': _L0_ffn_in['gate_w'], 'L0_ffn_up_w': _L0_ffn_in['up_w'], 'L0_ffn_down_w': _L0_ffn_in['down_w'], 'L1_xattn_Wq': _L1_xattn_in['Wq'], 'L1_xattn_bq': _L1_xattn_in['bq'], 'L1_xattn_Wk': _L1_xattn_in['Wk'], 'L1_xattn_bk': _L1_xattn_in['bk'], 'L1_xattn_Wv': _L1_xattn_in['Wv'], 'L1_xattn_bv': _L1_xattn_in['bv'], 'L1_xattn_Wo': _L1_xattn_in['Wo'], 'L1_xattn_bo': _L1_xattn_in['bo'], 'L1_xattn_scale': _L1_xattn_in['scale'], 'L1_ffn_wqkv': _L1_ffn_in['wqkv'], 'L1_ffn_q_scale': _L1_ffn_in['q_scale'], 'L1_ffn_k_scale': _L1_ffn_in['k_scale'], 'L1_ffn_wo': _L1_ffn_in['wo'], 'L1_ffn_ln_g': _L1_ffn_in['ln_g'], 'L1_ffn_ln_b': _L1_ffn_in['ln_b'], 'L1_ffn_w1': _L1_ffn_in['w1'], 'L1_ffn_b1': _L1_ffn_in['b1'], 'L1_ffn_w2': _L1_ffn_in['w2'], 'L1_ffn_b2': _L1_ffn_in['b2']}

def reference(x, ctx_768, mask_BxS2_bk0, L0_xattn_ln_x_g, L0_xattn_ln_x_b, L0_xattn_ln_l_g, L0_xattn_ln_l_b, L0_xattn_qn_g, L0_xattn_kn_g, L0_xattn_Wq, L0_xattn_Wkv, L0_xattn_Wlkv, L0_xattn_Wo, L0_xattn_bo, L0_ffn_macro_w, L0_ffn_micro_w, L0_ffn_gate_w, L0_ffn_up_w, L0_ffn_down_w, L1_xattn_Wq, L1_xattn_bq, L1_xattn_Wk, L1_xattn_bk, L1_xattn_Wv, L1_xattn_bv, L1_xattn_Wo, L1_xattn_bo, L1_xattn_scale, L1_ffn_wqkv, L1_ffn_q_scale, L1_ffn_k_scale, L1_ffn_wo, L1_ffn_ln_g, L1_ffn_ln_b, L1_ffn_w1, L1_ffn_b1, L1_ffn_w2, L1_ffn_b2):
    import jax
    import jax.numpy as jnp

    def _L0_xattn_ref(x, latents, mask, ln_x_g, ln_x_b, ln_l_g, ln_l_b, qn_g, kn_g, Wq, Wkv, Wlkv, Wo, bo):
        import jax, jax.numpy as jnp
        import numpy as np
        DIM_IN, DIM_LAT, DIM_HEAD = (192, 256, 64)
        INNER = max(DIM_LAT, DIM_IN)
        HEADS = INNER // DIM_HEAD
        SCALE = DIM_HEAD ** (-0.5)
        RMS_EPS = 1e-08
        LN_EPS = 1e-05

        def layernorm(x, g, b):
            mu = jnp.mean(x, axis=-1, keepdims=True)
            var = jnp.mean((x - mu) ** 2, axis=-1, keepdims=True)
            return (x - mu) * jax.lax.rsqrt(var + LN_EPS) * g + b

        def rmsnorm(x, gamma):
            norm = jnp.sqrt(jnp.sum(x * x, axis=-1, keepdims=True)) * x.shape[-1] ** (-0.5)
            return x / jnp.maximum(norm, RMS_EPS) * gamma
        b, n, _ = x.shape
        m = latents.shape[1]
        xn = layernorm(x, ln_x_g, ln_x_b)
        ln = layernorm(latents, ln_l_g, ln_l_b)
        q = ln @ Wq.T
        kv = jnp.concatenate([xn @ Wkv.T, ln @ Wlkv.T], axis=1)
        k, v = (kv[..., :INNER], kv[..., INNER:])
        split_heads = lambda t: t.reshape(t.shape[0], t.shape[1], HEADS, DIM_HEAD).transpose(0, 2, 1, 3)
        q, k, v = (split_heads(q), split_heads(k), split_heads(v))
        qn = rmsnorm(q, qn_g) * SCALE
        kn = rmsnorm(k, kn_g)
        attn = jnp.einsum('bhid,bhjd->bhij', qn, kn)
        full_mask = jnp.pad(mask, ((0, 0), (0, m)), constant_values=True)
        attn = jnp.where(full_mask[:, None, None, :], attn, -jnp.finfo(attn.dtype).max)
        attn = jax.nn.softmax(attn, axis=-1)
        out = jnp.einsum('bhij,bhjd->bhid', attn, v)
        out = out.transpose(0, 2, 1, 3).reshape(b, m, INNER)
        return out @ Wo.T + bo

    def _L0_ffn_ref(x, macro_w, micro_w, gate_w, up_w, down_w):
        import jax, jax.numpy as jnp
        import numpy as np
        D_MODEL = 256
        FFN_DIM = 512
        NUM_EXPERTS = 8
        NUM_GROUPS = 4
        EXPERTS_PER_GROUP = NUM_EXPERTS // NUM_GROUPS
        TOP_K = 2
        GROUPS_TOP_K = 1
        EPS = 1e-09

        def _topk_normalized(scores, k):
            vals, idx = jax.lax.top_k(scores, k)
            vals = vals / (jnp.sum(vals, axis=-1, keepdims=True) + EPS)
            return (vals, idx)
        B, S, D = x.shape
        T = B * S
        xf = x.reshape(T, D)
        macro_scores = jax.nn.sigmoid(xf @ macro_w)
        mv, mi = _topk_normalized(macro_scores, GROUPS_TOP_K)
        macro_full = jnp.sum(jax.nn.one_hot(mi, NUM_GROUPS, dtype=xf.dtype) * mv[..., None], axis=1)
        micro_scores = jax.nn.sigmoid(jnp.einsum('td,gde->tge', xf, micro_w))
        uv, ui = _topk_normalized(micro_scores, TOP_K)
        micro_full = jnp.sum(jax.nn.one_hot(ui, EXPERTS_PER_GROUP, dtype=xf.dtype) * uv[..., None], axis=2)
        w = (macro_full[:, :, None] * micro_full).reshape(T, NUM_EXPERTS)
        gate = jax.nn.silu(jnp.einsum('td,edf->tef', xf, gate_w))
        up = jnp.einsum('td,edf->tef', xf, up_w)
        h = gate * up
        out = jnp.einsum('te,tef,efd->td', w, h, down_w)
        return out.reshape(B, S, D)

    def _L1_xattn_ref(q, kv, Wq, bq, Wk, bk, Wv, bv, Wo, bo, scale):
        import jax, jax.numpy as jnp
        import numpy as np
        B, LQ, LKV = (4, 128, 512)
        DQ, DKV, H = (256, 192, 16)
        HD = DQ // H
        b, lq, _ = q.shape
        lkv = kv.shape[1]
        qh = (q @ Wq + bq).reshape(b, lq, H, HD).transpose(0, 2, 1, 3)
        kh = (kv @ Wk + bk).reshape(b, lkv, H, HD).transpose(0, 2, 1, 3)
        vh = (kv @ Wv + bv).reshape(b, lkv, H, HD).transpose(0, 2, 1, 3)
        scores = jnp.einsum('bhqd,bhkd->bhqk', qh, kh) * scale[0]
        attn = jax.nn.softmax(scores, axis=-1)
        out = jnp.einsum('bhqk,bhkd->bhqd', attn, vh)
        out = out.transpose(0, 2, 1, 3).reshape(b, lq, DQ)
        return out @ Wo + bo

    def _L1_ffn_ref(x, wqkv, q_scale, k_scale, wo, ln_g, ln_b, w1, b1, w2, b2):
        import jax, jax.numpy as jnp
        import numpy as np
        DIM = 256
        DEPTH = 2
        HEADS = 8
        DIM_HEAD = 64
        WINDOW = 128
        INNER = HEADS * DIM_HEAD
        HID = int(DIM * 4 * 2 / 3)
        B, N = (2, 2048)
        QK_SCALE = 8.0

        def shift_token(t):
            t1, t2 = jnp.split(t, 2, axis=-1)
            t2 = jnp.pad(t2, ((0, 0), (1, 0), (0, 0)))[:, :-1]
            return jnp.concatenate([t1, t2], axis=-1)

        def l2norm(t):
            return t / jnp.clip(jnp.linalg.norm(t, axis=-1, keepdims=True), 1e-12)

        def rotate_half(x):
            x1, x2 = jnp.split(x, 2, axis=-1)
            return jnp.concatenate([-x2, x1], axis=-1)

        def rotary_xpos(q, k):
            n = q.shape[-2]
            half_idx = jnp.arange(0, DIM_HEAD, 2, dtype=jnp.float32)
            inv_freq = 1.0 / 10000.0 ** (half_idx / DIM_HEAD)
            t = jnp.arange(n, dtype=jnp.float32)
            freqs = t[:, None] * inv_freq[None, :]
            freqs = jnp.concatenate([freqs, freqs], axis=-1)
            base = (half_idx + 0.4 * DIM_HEAD) / (1.4 * DIM_HEAD)
            power = (t - n // 2) / float(WINDOW // 2)
            scale = base[None, :] ** power[:, None]
            scale = jnp.concatenate([scale, scale], axis=-1)
            cos, sin = (jnp.cos(freqs), jnp.sin(freqs))
            q = q * cos * scale + rotate_half(q) * sin * scale
            k = k * cos / scale + rotate_half(k) * sin / scale
            return (q, k)

        def local_attention(q, k, v):
            b, h, n, d = q.shape
            w = n // WINDOW
            bq = q.reshape(b, h, w, WINDOW, d) * QK_SCALE
            bk = k.reshape(b, h, w, WINDOW, d)
            bv = v.reshape(b, h, w, WINDOW, d)

            def look_around(t):
                p = jnp.pad(t, ((0, 0), (0, 0), (1, 0), (0, 0), (0, 0)))
                return jnp.concatenate([p[:, :, :w], p[:, :, 1:]], axis=3)
            bk, bv = (look_around(bk), look_around(bv))
            bt = jnp.arange(n).reshape(w, WINDOW)
            btp = jnp.pad(bt, ((1, 0), (0, 0)), constant_values=-1)
            btk = jnp.concatenate([btp[:w], btp[1:]], axis=1)
            sim = jnp.einsum('bhwid,bhwjd->bhwij', bq, bk)
            i = bt[:, :, None]
            j = btk[:, None, :]
            mask = (i < j) | (i > j + WINDOW) | (j == -1)
            sim = jnp.where(mask, -jnp.finfo(sim.dtype).max, sim)
            attn = jax.nn.softmax(sim, axis=-1)
            out = jnp.einsum('bhwij,bhwjd->bhwid', attn, bv)
            return out.reshape(b, h, n, d)

        def _layer(x, wqkv, qs, ksc, wo, lg, lb, w1, b1, w2, b2):
            b, n, _ = x.shape
            h = shift_token(x)
            qkv = h @ wqkv
            q, k, v = jnp.split(qkv, 3, axis=-1)
            to_heads = lambda t: t.reshape(b, n, HEADS, DIM_HEAD).transpose(0, 2, 1, 3)
            q, k, v = (to_heads(q), to_heads(k), to_heads(v))
            q = l2norm(q) * qs
            k = l2norm(k) * ksc
            q, k = rotary_xpos(q, k)
            o = local_attention(q, k, v)
            o = o.transpose(0, 2, 1, 3).reshape(b, n, INNER)
            x = x + o @ wo
            h = shift_token(x)
            mu = h.mean(-1, keepdims=True)
            var = h.var(-1, keepdims=True)
            h = (h - mu) / jnp.sqrt(var + 1e-05) * lg + lb
            h = h @ w1 + b1
            a, g = jnp.split(h, 2, axis=-1)
            h = a * jax.nn.gelu(g, approximate=False)
            x = x + h @ w2 + b2
            return x
        for l in range(DEPTH):
            x = _layer(x, wqkv[l], q_scale[l], k_scale[l], wo[l], ln_g[l], ln_b[l], w1[l], b1[l], w2[l], b2[l])
        return x
    x = x + _L0_xattn_ref(ctx_768, _layernorm(x, axis=-1), mask_BxS2_bk0, L0_xattn_ln_x_g, L0_xattn_ln_x_b, L0_xattn_ln_l_g, L0_xattn_ln_l_b, L0_xattn_qn_g, L0_xattn_kn_g, L0_xattn_Wq, L0_xattn_Wkv, L0_xattn_Wlkv, L0_xattn_Wo, L0_xattn_bo)
    x = x + _L0_ffn_ref(_layernorm(x, axis=-1), L0_ffn_macro_w, L0_ffn_micro_w, L0_ffn_gate_w, L0_ffn_up_w, L0_ffn_down_w)
    x = x + _L1_xattn_ref(_layernorm(x, axis=-1), ctx_768, L1_xattn_Wq, L1_xattn_bq, L1_xattn_Wk, L1_xattn_bk, L1_xattn_Wv, L1_xattn_bv, L1_xattn_Wo, L1_xattn_bo, L1_xattn_scale)
    x = x + _L1_ffn_ref(_layernorm(x, axis=-1), L1_ffn_wqkv, L1_ffn_q_scale, L1_ffn_k_scale, L1_ffn_wo, L1_ffn_ln_g, L1_ffn_ln_b, L1_ffn_w1, L1_ffn_b1, L1_ffn_w2, L1_ffn_b2)
    return x

_drawn_inputs = setup_inputs


def setup_inputs(seed=0):
    import zlib

    import numpy as np

    out = dict(_drawn_inputs(seed))
    spreads = {'L0_xattn_ln_x_g': (1.0, 0.6),
     'L0_xattn_ln_x_b': (0.0, 0.8),
     'L0_xattn_ln_l_g': (1.0, 0.2),
     'L0_xattn_ln_l_b': (0.0, 0.1),
     'L0_xattn_qn_g': (1.0, 0.6),
     'L0_xattn_kn_g': (1.0, 0.6),
     'L0_xattn_bo': (0.0, 0.1),
     'L1_xattn_bq': (0.0, 2.0),
     'L1_xattn_bk': (0.0, 2.0),
     'L1_xattn_bv': (0.0, 0.1),
     'L1_xattn_bo': (0.0, 0.1),
     'L1_ffn_q_scale': (1.0, 0.6),
     'L1_ffn_k_scale': (1.0, 0.6),
     'L1_ffn_ln_g': (1.0, 0.6),
     'L1_ffn_ln_b': (0.0, 0.8),
     'L1_ffn_b1': (0.0, 0.8),
     'L1_ffn_b2': (0.0, 0.1)}
    factors = {'L0_xattn_Wkv': 3.675,
     'L0_ffn_macro_w': 4.379,
     'L0_ffn_micro_w': 8.0,
     'L0_ffn_gate_w': 3.821,
     'L0_ffn_up_w': 3.777,
     'L0_ffn_down_w': 3.773}
    for name, (base, spread) in spreads.items():
        noise = np.random.default_rng([zlib.crc32(name.encode()), seed]).standard_normal(out[name].shape)
        drawn = base * np.exp(spread * noise) if base else spread * noise
        out[name] = jnp.asarray(drawn.astype(out[name].dtype))
    for name, factor in factors.items():
        out[name] = (out[name] * factor).astype(out[name].dtype)
    return out
```

```python
from contextlib import ExitStack

import concourse.bass as bass
from concourse import mybir

ALU = mybir.AluOpType
ACT = mybir.ActivationFunctionType
AX_X = mybir.AxisListType.X
F32 = mybir.dt.float32
I32 = mybir.dt.int32

P = 128
BATCH, SEQ, D = 4, 1024, 256
NTOK = BATCH * SEQ
DC = D // P
TPB = SEQ // P
NT = NTOK // P
S = 4
NCTX, DCTX = 154, 192
CC = DCTX // 2
TAIL = NCTX - P
TPAD = 32
H0, HD0 = 4, 64
KEYS0 = SEQ + NCTX
KC0 = TPB + 2
H1, HD1 = 16, 16
V1W = HD1 + 1
V1 = H1 * V1W
MGROUPS, EXPERTS, FFN = 4, 8, 512
NR = MGROUPS + EXPERTS
NTS = NT + MGROUPS
XW = D + 2
HL, HDL, DEPTH = 8, 64, 2
HIDDEN, HC = 682, 6
HCW = (HIDDEN + HC - 1) // HC
EPS = 1e-5
BIG = 1e30


class Semaphores:

    def __init__(self, nc):
        self.nc, self.taken = nc, []

    def take(self, name):
        self.taken.append(self.nc.alloc_semaphore(name))
        return self.taken[-1]

    def release(self):
        self.nc.clear_and_free_semaphores(self.taken)
        self.nc.all_engine_barrier()


class Signal:

    def __init__(self, sem, per, unit=1, ahead=1):
        self.sem, self.per, self.unit, self.ahead = sem, per, unit, ahead

    def start(self, eng):
        eng.sem_inc(self.sem, self.per * self.unit * self.ahead)

    def back(self, i, n, passes):
        return i * (self.per * self.unit) + (self.per * (self.ahead - passes) + n + 1) * self.unit

    def now(self, i, n):
        return self.back(i, n, 0)

    def prev(self, i, n):
        return self.back(i, n, 1)


class Steps:

    def __init__(self, sem, per):
        self.sem, self.per, self.n = sem, per, 0

    def mark(self):
        self.n += 1
        return self.sem, 1

    def last(self, i):
        return i * self.per + self.n

    def done(self):
        assert self.n == self.per, (self.n, self.per)
        self.n = 0


def keys_and_projections(nc, c, x, ctx, w, scratch):
    sems = Semaphores(nc)
    with ExitStack() as es:
        def sb(name, shape, dt=F32):
            return es.enter_context(nc.sbuf_tensor("s1_" + name, shape, dt))

        def sem(name):
            return sems.take("s1_" + name)

        def sig(name, per, unit=1):
            return Signal(sem(name), per, unit)

        ident = c["ident"]
        B = 2
        wl = sb("wl", [P, DC, 3 * D])
        wkv = sb("wkv", [CC, 2, 2 * D])
        wk1 = sb("wk1", [CC, 2, D])
        wv1 = sb("wv1", [CC, 2, D])
        bv1 = sb("bv1", [P, D])
        cols = sb("cols", [P, 10])
        gl, bl, bk1 = cols[:, 0:2], cols[:, 2:4], cols[:, 4:6]
        gq, gk = cols[:, 6:7], cols[:, 7:8]
        gx = sb("gx", [CC, 4])
        mhalf = sb("mhalf", [P, 8])
        eps = sb("eps", [P, S])
        gqs = sb("gqs", [P, 1])
        C = sb("C", [P, B, 2, DCTX])
        Cn = sb("Cn", [P, B, 2, DCTX])
        CT = sb("CT", [CC, B, 2, 2 * P])
        CnT = sb("CnT", [CC, B, 2, 2 * P])
        CTail = sb("CTail", [CC, B, 2, 4, TPAD])
        cstat = sb("cstat", [P, B, 2, 6])
        cmv = sb("cmv", [P, B, 2, 2])
        crs = sb("crs", [P, B, 2, 2])
        csq = sb("csq", [P, B, 2, D])
        css = sb("css", [P, B, 2, 4])
        csr1 = sb("csr1", [P, B, 2, 4])
        Kn = sb("Kn", [P, B, 2, D])
        KT0 = sb("KT0", [P, B, 2, 2 * P])
        VC = sb("VC", [P, B, 2, D])
        KT1 = sb("KT1", [P, B, 2, 2 * P])
        VV = sb("VV", [P, B, 2, V1])
        X = sb("X", [P, S, D])
        Y = sb("Y", [P, S, D])
        Z = sb("Z", [P, S, D])
        fence = sb("fence", [P, 1])
        st = sb("st", [P, S, 2, 6])
        mv = sb("mv", [P, S, 2, 2])
        rs = sb("rs", [P, S, 2, 2])
        LT = sb("LT", [P, S, DC, P])
        sq = sb("sq", [P, S, 2 * D])
        ss = sb("ss", [P, S, 8])
        sr = sb("sr", [P, S, 8])
        QKn = sb("QKn", [P, S, 2 * D])
        QT = sb("QT", [P, S, DC, P])
        KT = sb("KT", [P, S, DC, P])
        V = sb("V", [P, S, D])
        A = [es.enter_context(nc.psum_tensor(f"s1_A{s}", [P, 512], F32)) for s in range(S)]
        Bk = [es.enter_context(nc.psum_tensor(f"s1_B{s}", [P, 512], F32)) for s in range(S)]

        consts = sem("consts")
        prep = sem("prep")
        prep2 = sem("exponent")
        prep3 = sem("value_frame")
        c_loaded = [sig(f"c_loaded{b}", 2, 16) for b in range(B)]
        c_stats = sig("c_stats", B)
        c_rstd = sig("c_rstd", B)
        c_norm = sig("c_norm", B)
        c_turned = sig("c_turned", B)
        c_evac = sig("c_evac", B)
        c_tail = sig("c_tail", B)
        c_kv = sig("c_kv", B)
        c_sq = sig("c_sq", B)
        c_ss = sig("c_ss", B)
        c_sr = sig("c_sr", B)
        c_kn = sig("c_kn", B)
        c_kturn = sig("c_kturn", B)
        c_k1 = sig("c_k1", B)
        c_kt0 = sig("c_kt0", B)
        c_kt1 = sig("c_kt1", B)
        c_v1 = sig("c_v1", B)
        c_vv = sig("c_vv", B)
        c_stored = [sig(f"c_stored{b}", 4, 16) for b in range(B)]
        x_loaded = [sig(f"x_loaded{s}", 1, 16) for s in range(S)]
        stats = sig("stats", 2 * S)
        rstd = sig("rstd", 2)
        z_ready = sig("z_ready", S)
        z_turned = sig("z_turned", S)
        lt_ready = sig("lt_ready", S)
        qkv_done = sig("qkv_done", S)
        sq_ready = sig("sq_ready", S)
        ss_ready = sig("ss_ready", S)
        sr_ready = sig("sr_ready", S)
        qkn_ready = sig("qkn_ready", S)
        qk_turned = sig("qk_turned", S)
        qkt_ready = sig("qkt_ready", S)
        stored = [sig(f"stored{s}", 3, 16) for s in range(S)]
        dve = Steps(sem("dve_steps"), 2 * B)
        dve2 = Steps(sem("dve_steps2"), 3 + S)
        dve0 = sem("dve_first_steps")
        pool0 = sem("pool_first_steps")
        pool = Steps(sem("pool_steps"), B)
        pool2 = Steps(sem("pool_steps2"), 2)
        NCONST = 8

        with nc.Block() as block:
            @block.sync
            def _(sp):
                for dst, src in ((c["ident"], w["ident"]), (wl, w["wl"]), (wkv, w["wkv"]), (wk1, w["wk1"]),
                                 (wv1, w["wv1"]), (cols, w["cols"]), (gx, w["gx"])):
                    sp.dma_start(dst[:], src).then_inc(consts, 16)
                sp.dma_start(bv1[:], w["bv1"].partition_broadcast(P)).then_inc(consts, 16)
                for b in range(B):
                    c_loaded[b].start(sp)
                    c_stored[b].start(sp)
                for s in range(S):
                    x_loaded[s].start(sp)
                    stored[s].start(sp)
                sp.wait_ge(prep, 1)
                with sp.Fori(0, BATCH // B) as i:
                    for b in range(B):
                        sp.wait_ge(c_turned.sem, c_turned.prev(i, b))
                        sp.dma_start(C[:, b, 0, :], ctx[bass.ds(i * B + b, 1), 0:P, :].rearrange("a p d -> (a p) d")).then_inc(c_loaded[b].sem, 16)
                        sp.dma_start(C[0:TAIL, b, 1, :], ctx[bass.ds(i * B + b, 1), P:NCTX, :].rearrange("a p d -> (a p) d")).then_inc(c_loaded[b].sem, 16)
                    for b in range(B):
                        sp.wait_ge(c_kt0.sem, c_kt0.now(i, b))
                        sp.dma_start(scratch["k0"][bass.ds(i * B + b, 1), :, :, SEQ:KEYS0].rearrange("a p c n -> (a p) c n"),
                                     KT0[:, b, :, 0:NCTX]).then_inc(c_stored[b].sem, 16)
                        sp.dma_start(scratch["v0"][bass.ds(i * B + b, 1), :, TPB:KC0, :].rearrange("a p c n -> (a p) c n"),
                                     VC[:, b, :, :]).then_inc(c_stored[b].sem, 16)
                        sp.wait_ge(c_kt1.sem, c_kt1.now(i, b))
                        sp.dma_start(scratch["k1"][bass.ds(i * B + b, 1), :, :, :].rearrange("a p c n -> (a p) c n"),
                                     KT1[:, b, :, 0:NCTX]).then_inc(c_stored[b].sem, 16)
                        sp.wait_ge(c_vv.sem, c_vv.now(i, b))
                        sp.dma_start(scratch["v1"][bass.ds(i * B + b, 1), :, :, :].rearrange("a p c n -> (a p) c n"),
                                     VV[:, b, :, :]).then_inc(c_stored[b].sem, 16)
                def load_x(i, s):
                    sp.dma_start(X[:, s, :], x[bass.ds(i * (S * P) + s * P, P), :]).then_inc(x_loaded[s].sem, 16)

                for s in range(S):
                    load_x(0, s)
                with sp.Fori(0, BATCH) as bb:
                    with sp.Fori(0, TPB // S) as h:
                        i = bb * (TPB // S) + h
                        for s in range(S):
                            sp.wait_ge(z_ready.sem, z_ready.now(i, s))
                            load_x((i + 1) % (NT // S), s)
                        for s in range(S):
                            sp.wait_ge(qkt_ready.sem, qkt_ready.now(i, s))
                            sp.dma_start(scratch["q0"][bass.ds(i * S + s, 1), :, :, :].rearrange("a p c n -> (a p) c n"),
                                         QT[:, s, :, :]).then_inc(stored[s].sem, 16)
                            sp.dma_start(scratch["k0"][bass.ds(bb, 1), :, :, bass.ds(h * (S * P) + s * P, P)].rearrange("a p c n -> (a p) c n"),
                                         KT[:, s, :, :]).then_inc(stored[s].sem, 16)
                            sp.dma_start(scratch["v0"][bass.ds(bb, 1), :, bass.ds(h * S + s, 1), :].rearrange("a p c n -> (a p) (c n)"),
                                         V[:, s, :]).then_inc(stored[s].sem, 16)
                for s in range(S):
                    sp.wait_ge(x_loaded[s].sem, x_loaded[s].now(NT // S, 0))
                for b in range(B):
                    sp.wait_ge(c_stored[b].sem, c_stored[b].now(BATCH // B - 1, 3))
                for s in range(S):
                    sp.wait_ge(stored[s].sem, stored[s].now(NT // S - 1, 2))

            @block.gpsimd
            def _(gp):
                for q in (c_rstd, c_sr, rstd, sr_ready):
                    q.start(gp)
                gp.memset(mhalf[:], -0.5).then_inc(prep2, 1)
                gp.memset(eps[:], EPS).then_inc(prep2, 1)
                gp.wait_ge(prep2, 2)
                with gp.Fori(0, BATCH // B) as i:
                    for b in range(B):
                        gp.wait_ge(c_stats.sem, c_stats.now(i, b))
                        gp.tensor_tensor(crs[:, b, :, 0], cmv[:, b, :, 1], eps[:, 0:2], ALU.add).then_inc(*pool.mark())
                        gp.wait_ge(pool.sem, pool.last(i))
                        gp.tensor_tensor(crs[:, b, :, 1], crs[:, b, :, 0], mhalf[:, 0:2], ALU.pow).then_inc(c_rstd.sem, 1)
                    for b in range(B):
                        gp.wait_ge(c_ss.sem, c_ss.now(i, b))
                        gp.tensor_tensor(csr1[:, b, :, :].rearrange("p a b -> p (a b)"), css[:, b, :, :].rearrange("p a b -> p (a b)"),
                                         mhalf[:, 0:8], ALU.pow).then_inc(c_sr.sem, 1)
                    pool.done()
                def inverse_deviations(i, k, mark, last):
                    gp.wait_ge(stats.sem, stats.now(i, k * S + S - 1))
                    gp.tensor_tensor(rs[:, :, k, 0], mv[:, :, k, 1], eps[:], ALU.add).then_inc(*mark())
                    gp.wait_ge(*last())
                    gp.tensor_tensor(rs[:, :, k, 1], rs[:, :, k, 0], mhalf[:, 0:S], ALU.pow).then_inc(rstd.sem, 1)

                def inverse_norms(i, s):
                    gp.wait_ge(ss_ready.sem, ss_ready.now(i, s))
                    gp.tensor_tensor(sr[:, s, :], ss[:, s, :], mhalf[:, 0:8], ALU.pow).then_inc(sr_ready.sem, 1)

                for k in range(2):
                    inverse_deviations(0, k, lambda: (pool0, 1), lambda k=k: (pool0, k + 1))
                with gp.Fori(0, NT // S - 1) as i:
                    last = lambda: (pool2.sem, pool2.last(i))
                    inverse_norms(i, 0)
                    inverse_deviations(i + 1, 0, pool2.mark, last)
                    inverse_norms(i, 1)
                    inverse_norms(i, 2)
                    inverse_deviations(i + 1, 1, pool2.mark, last)
                    inverse_norms(i, 3)
                    pool2.done()
                for s in range(S):
                    inverse_norms(NT // S - 1, s)

            @block.vector
            def _(v):
                for q in (c_stats, c_norm, c_tail, c_ss, c_kn, c_kt1, c_vv, stats, z_ready, ss_ready, qkn_ready):
                    q.start(v)
                v.memset(C[:], 0.0).then_inc(prep, 1)
                v.memset(VV[:], 0.0).then_inc(prep3, 1)
                v.wait_ge(prep3, 1)
                v.memset(VV[:, :, 0, :].rearrange("p b (h w) -> p b h w", w=V1W)[:, :, :, HD1:V1W], 1.0).then_inc(prep3, 1)
                for g in range(4):
                    v.memset(VV[g * TPAD:(g + 1) * TPAD, :, 1, :].rearrange("p b (t w) -> p b t w", w=4 * V1W)
                             [:, :, :, g * V1W + HD1:(g + 1) * V1W], 1.0).then_inc(prep3, 1)
                v.wait_ge(consts, 16 * NCONST)
                v.tensor_scalar(gqs[:], gq, HD0 ** -0.5, None, ALU.mult).then_inc(prep3, 1)
                v.wait_ge(prep3, 7)
                with v.Fori(0, BATCH // B) as i:
                    for b in range(B):
                        v.wait_ge(c_loaded[b].sem, c_loaded[b].now(i, 1))
                        v.bn_stats(cstat[:, b, 0, :], C[:, b, 0, :])
                        v.bn_stats(cstat[:, b, 1, :], C[:, b, 1, :]).then_inc(*dve.mark())
                        v.wait_ge(dve.sem, dve.last(i))
                        v.memset(fence[:], 0.0)
                        v.bn_aggr(cmv[:, b, 0, :], cstat[:, b, 0, :])
                        v.bn_aggr(cmv[:, b, 1, :], cstat[:, b, 1, :]).then_inc(c_stats.sem, 1)
                    for b in range(B):
                        v.wait_ge(c_rstd.sem, c_rstd.now(i, b))
                        v.tensor_scalar(Cn[:, b, 0, :], C[:, b, 0, :], cmv[:, b, 0, 0:1], crs[:, b, 0, 1:2], ALU.subtract, ALU.mult)
                        v.tensor_scalar(Cn[:, b, 1, :], C[:, b, 1, :], cmv[:, b, 1, 0:1], crs[:, b, 1, 1:2], ALU.subtract, ALU.mult).then_inc(c_norm.sem, 1)
                    for b in range(B):
                        v.wait_ge(c_evac.sem, c_evac.now(i, b))
                        for k in range(2):
                            ins = v.tensor_copy(CTail[:, b, k, :, :], CT[:, b, k, P:P + TPAD].unsqueeze(1).to_broadcast([CC, 4, TPAD]))
                        ins.then_inc(c_tail.sem, 1)
                    for b in range(B):
                        v.wait_ge(c_sq.sem, c_sq.now(i, b))
                        v.tensor_reduce(css[:, b, :, :], csq[:, b, :, :].rearrange("p a (h d) -> p a h d", d=HD0), AX_X, ALU.add).then_inc(*dve.mark())
                        v.wait_ge(dve.sem, dve.last(i))
                        v.tensor_scalar(css[:, b, :, :], css[:, b, :, :], 1e-16, None, ALU.max).then_inc(c_ss.sem, 1)
                    for b in range(B):
                        v.wait_ge(c_sr.sem, c_sr.now(i, b))
                        for k, bank in enumerate((A[b], Bk[b])):
                            ins = v.tensor_tensor(Kn[:, b, k, :].rearrange("p (h d) -> p h d", d=HD0), bank[:, 0:D].rearrange("p (h d) -> p h d", d=HD0),
                                                  csr1[:, b, k, :].unsqueeze(2).to_broadcast([P, H0, HD0]), ALU.mult)
                        ins.then_inc(c_kn.sem, 1)
                    for b in range(B):
                        v.wait_ge(c_k1.sem, c_k1.now(i, b))
                        v.wait_ge(c_stored[b].sem, c_stored[b].prev(i, 3))
                        for k in range(2):
                            ins = v.tensor_scalar(KT1[:, b, k, :], Bk[b][:, k * 256:(k + 1) * 256], bk1[:, k:k + 1], None, ALU.add)
                        ins.then_inc(c_kt1.sem, 1)
                    for b in range(B):
                        v.wait_ge(c_v1.sem, c_v1.now(i, b))
                        v.tensor_tensor(VV[:, b, 0, :].rearrange("p (h w) -> p h w", w=V1W)[:, :, 0:HD1], A[b][:, 0:D].rearrange("p (h d) -> p h d", d=HD1),
                                        bv1[:].rearrange("p (h d) -> p h d", d=HD1), ALU.add)
                        for g in range(4):
                            rows = slice(g * TPAD, (g + 1) * TPAD)
                            ins = v.tensor_tensor(VV[rows, b, 1, :].rearrange("p (t w) -> p t w", w=4 * V1W)[:, :, g * V1W:g * V1W + HD1],
                                                  A[b][rows, D:2 * D].rearrange("p (t w) -> p t w", w=4 * HD1)[:, :, g * HD1:(g + 1) * HD1],
                                                  bv1[rows, :].rearrange("p (t w) -> p t w", w=4 * HD1)[:, :, g * HD1:(g + 1) * HD1], ALU.add)
                        ins.then_inc(c_vv.sem, 1)
                    dve.done()
                def first_stats(i, mark, last):
                    for s in range(S):
                        v.wait_ge(x_loaded[s].sem, x_loaded[s].now(i, 0))
                        ins = v.bn_stats(st[:, s, 0, :], X[:, s, :])
                    ins.then_inc(*mark())
                    v.wait_ge(*last())
                    v.memset(fence[:], 0.0)
                    for s in range(S):
                        v.bn_aggr(mv[:, s, 0, :], st[:, s, 0, :]).then_inc(stats.sem, 1)

                def first_norm(i, mark, last):
                    v.wait_ge(rstd.sem, rstd.now(i, 0))
                    for s in range(S):
                        ins = v.tensor_scalar(Y[:, s, :], X[:, s, :], mv[:, s, 0, 0:1], rs[:, s, 0, 1:2], ALU.subtract, ALU.mult)
                    ins.then_inc(*mark())
                    return last()

                def second_stats(normed, mark, last):
                    v.wait_ge(*normed)
                    for s in range(S):
                        ins = v.bn_stats(st[:, s, 1, :], Y[:, s, :])
                    ins.then_inc(*mark())
                    v.wait_ge(*last())
                    v.memset(fence[:], 0.0)
                    for s in range(S):
                        v.bn_aggr(mv[:, s, 1, :], st[:, s, 1, :]).then_inc(stats.sem, 1)

                def second_norm(i):
                    v.wait_ge(rstd.sem, rstd.now(i, 1))
                    for s in range(S):
                        v.wait_ge(z_turned.sem, z_turned.prev(i, s))
                        v.tensor_scalar(Z[:, s, :], Y[:, s, :], mv[:, s, 1, 0:1], rs[:, s, 1, 1:2], ALU.subtract, ALU.mult).then_inc(z_ready.sem, 1)

                def sum_squares(i, s, last):
                    v.wait_ge(sq_ready.sem, sq_ready.now(i, s))
                    v.tensor_reduce(ss[:, s, :], sq[:, s, :].rearrange("p (h d) -> p h d", d=HD0), AX_X, ALU.add).then_inc(*dve2.mark())
                    v.wait_ge(*last())
                    v.tensor_scalar(ss[:, s, :], ss[:, s, :], 1e-16, None, ALU.max).then_inc(ss_ready.sem, 1)

                def normalize(i, s):
                    v.wait_ge(sr_ready.sem, sr_ready.now(i, s))
                    v.tensor_tensor(QKn[:, s, :].rearrange("p (h d) -> p h d", d=HD0), A[s][:].rearrange("p (h d) -> p h d", d=HD0),
                                    sr[:, s, :].unsqueeze(2).to_broadcast([P, 8, HD0]), ALU.mult).then_inc(qkn_ready.sem, 1)

                first = Steps(dve0, 3)
                last = lambda: (dve0, first.last(0))
                first_stats(0, first.mark, last)
                second_stats(first_norm(0, first.mark, last), first.mark, last)
                second_norm(0)
                with v.Fori(0, NT // S - 1) as i:
                    last = lambda: (dve2.sem, dve2.last(i))
                    sum_squares(i, 0, last)
                    first_stats(i + 1, dve2.mark, last)
                    sum_squares(i, 1, last)
                    normed = first_norm(i + 1, dve2.mark, last)
                    normalize(i, 0)
                    sum_squares(i, 2, last)
                    second_stats(normed, dve2.mark, last)
                    normalize(i, 1)
                    sum_squares(i, 3, last)
                    normalize(i, 2)
                    second_norm(i + 1)
                    normalize(i, 3)
                    dve2.done()
                last = lambda: (dve2.sem, dve2.last(NT // S - 1))
                for s in range(S):
                    sum_squares(NT // S - 1, s, last)
                for s in range(S):
                    normalize(NT // S - 1, s)

            @block.scalar
            def _(a):
                for q in (c_evac, c_sq, c_kt0, lt_ready, sq_ready, qkt_ready):
                    q.start(a)
                a.wait_ge(consts, 16 * NCONST)
                a.wait_ge(prep3, 7)
                with a.Fori(0, BATCH // B) as i:
                    for b in range(B):
                        a.wait_ge(c_turned.sem, c_turned.now(i, b))
                        for k in range(2):
                            a.activation(CnT[:, b, k, :], A[b][0:CC, k * 256:(k + 1) * 256], ACT.Identity, scale=gx[:, k:k + 1], bias=gx[:, 2 + k:3 + k])
                        a.copy(CT[:, b, :, :].rearrange("p a b -> p (a b)"), Bk[b][0:CC, :]).then_inc(c_evac.sem, 1)
                    for b in range(B):
                        a.wait_ge(c_kv.sem, c_kv.now(i, b))
                        a.wait_ge(c_stored[b].sem, c_stored[b].prev(i, 3))
                        for k, bank in enumerate((A[b], Bk[b])):
                            a.copy(VC[:, b, k, :], bank[:, D:2 * D])
                            ins = a.activation(csq[:, b, k, :], bank[:, 0:D], ACT.Square, scale=HD0 ** -0.5)
                        ins.then_inc(c_sq.sem, 1)
                    for b in range(B):
                        a.wait_ge(c_kturn.sem, c_kturn.now(i, b))
                        a.activation(KT0[:, b, :, :].rearrange("p a b -> p (a b)"), A[b][:], ACT.Copy, scale=gk).then_inc(c_kt0.sem, 1)
                def latents(i):
                    for s in range(S):
                        a.wait_ge(z_turned.sem, z_turned.now(i, s))
                        for k in range(DC):
                            ins = a.activation(LT[:, s, k, :], Bk[s][:, k * P:(k + 1) * P], ACT.Identity, scale=gl[:, k:k + 1], bias=bl[:, k:k + 1])
                        ins.then_inc(lt_ready.sem, 1)

                def values(i, s):
                    a.wait_ge(qkv_done.sem, qkv_done.now(i, s))
                    a.wait_ge(stored[s].sem, stored[s].prev(i, 2))
                    a.activation(sq[:, s, :], A[s][:], ACT.Square, scale=HD0 ** -0.5)
                    a.copy(V[:, s, :], Bk[s][:, 0:D]).then_inc(sq_ready.sem, 1)

                def queries_keys(i, s):
                    a.wait_ge(qk_turned.sem, qk_turned.now(i, s))
                    a.activation(QT[:, s, :, :].rearrange("p a b -> p (a b)"), A[s][:, 0:D], ACT.Copy, scale=gqs[:])
                    a.activation(KT[:, s, :, :].rearrange("p a b -> p (a b)"), A[s][:, D:2 * D], ACT.Copy, scale=gk).then_inc(qkt_ready.sem, 1)

                latents(0)
                with a.Fori(0, NT // S - 1) as i:
                    for s in range(S):
                        values(i, s)
                    for s in range(S):
                        queries_keys(i, s)
                    latents(i + 1)
                for s in range(S):
                    values(NT // S - 1, s)
                for s in range(S):
                    queries_keys(NT // S - 1, s)

            @block.tensor
            def _(pe):
                for q in (c_turned, c_kv, c_kturn, c_k1, c_v1, z_turned, qkv_done, qk_turned):
                    q.start(pe)
                pe.wait_ge(consts, 16 * NCONST)
                with pe.Fori(0, BATCH // B) as i:
                    for b in range(B):
                        pe.wait_ge(c_norm.sem, c_norm.now(i, b))
                        pe.wait_ge(c_vv.sem, c_vv.prev(i, b))
                        for src, bank in ((Cn, A[b]), (C, Bk[b])):
                            for r in range(2):
                                for k in range(2):
                                    ins = pe.transpose(bank[0:CC, k * 256 + r * P:k * 256 + (r + 1) * P], src[:, b, r, k * CC:(k + 1) * CC], ident[:])
                        ins.then_inc(c_turned.sem, 1)
                    for b in range(B):
                        pe.wait_ge(c_evac.sem, c_evac.now(i, b))
                        for r, bank in enumerate((A[b], Bk[b])):
                            for k in range(2):
                                ins = pe.matmul(bank[:], CnT[:, b, k, r * P:(r + 1) * P], wkv[:, k, :], start=(k == 0), stop=(k == 1))
                        ins.then_inc(c_kv.sem, 1)
                    for b in range(B):
                        pe.wait_ge(c_kn.sem, c_kn.now(i, b))
                        for r in range(2):
                            for k in range(2):
                                ins = pe.transpose(A[b][:, k * 256 + r * P:k * 256 + (r + 1) * P], Kn[:, b, r, k * P:(k + 1) * P], ident[:])
                        ins.then_inc(c_kturn.sem, 1)
                    for b in range(B):
                        for m in range(2):
                            for k in range(2):
                                ins = pe.matmul(Bk[b][:, m * 256:(m + 1) * 256], wk1[:, k, m * P:(m + 1) * P], CT[:, b, k, :], start=(k == 0), stop=(k == 1))
                        ins.then_inc(c_k1.sem, 1)
                    for b in range(B):
                        pe.wait_ge(c_kt0.sem, c_kt0.now(i, b))
                        pe.wait_ge(c_tail.sem, c_tail.now(i, b))
                        for k in range(2):
                            pe.matmul(A[b][:, 0:D], CT[:, b, k, 0:P], wv1[:, k, :], start=(k == 0), stop=(k == 1))
                        for k in range(2):
                            ins = pe.matmul(A[b][:, D:2 * D], CTail[:, b, k, :, :].rearrange("p a b -> p (a b)"), wv1[:, k, :], start=(k == 0), stop=(k == 1))
                        ins.then_inc(c_v1.sem, 1)
                pe.wait_ge(c_vv.sem, c_vv.now(BATCH // B - 1, B - 1))
                def turn_z(i):
                    for s in range(S):
                        pe.wait_ge(z_ready.sem, z_ready.now(i, s))
                        pe.wait_ge(sq_ready.sem, sq_ready.prev(i, s))
                        for k in range(DC):
                            ins = pe.transpose(Bk[s][:, k * P:(k + 1) * P], Z[:, s, k * P:(k + 1) * P], ident[:])
                        ins.then_inc(z_turned.sem, 1)

                def project(i):
                    for s in range(S):
                        pe.wait_ge(lt_ready.sem, lt_ready.now(i, s))
                        pe.wait_ge(qkt_ready.sem, qkt_ready.prev(i, s))
                        for k in range(DC):
                            pe.matmul(A[s][:], LT[:, s, k, :], wl[:, k, 0:2 * D], start=(k == 0), stop=(k == DC - 1))
                        for k in range(DC):
                            ins = pe.matmul(Bk[s][:, 0:D], LT[:, s, k, :], wl[:, k, 2 * D:3 * D], start=(k == 0), stop=(k == DC - 1))
                        ins.then_inc(qkv_done.sem, 1)

                def turn_qk(i, s):
                    pe.wait_ge(qkn_ready.sem, qkn_ready.now(i, s))
                    for k in range(4):
                        ins = pe.transpose(A[s][:, k * P:(k + 1) * P], QKn[:, s, k * P:(k + 1) * P], ident[:])
                    ins.then_inc(qk_turned.sem, 1)

                turn_z(0)
                with pe.Fori(0, NT // S - 1) as i:
                    project(i)
                    for s in range(3):
                        turn_qk(i, s)
                    turn_z(i + 1)
                    turn_qk(i, 3)
                project(NT // S - 1)
                for s in range(S):
                    turn_qk(NT // S - 1, s)
    sems.release()


def attention0(nc, c, x, w, scratch):
    S = TPB
    HEADS = S * H0
    GROUPS = ((0, 4), (4, 8), (8, KC0))
    sems = Semaphores(nc)
    with ExitStack() as es:
        def sb(name, shape, dt=F32):
            return es.enter_context(nc.sbuf_tensor("s2_" + name, shape, dt))

        def sem(name):
            return sems.take("s2_" + name)

        def sig(name, per, unit=1, ahead=1):
            return Signal(sem(name), per, unit, ahead)

        ident = c["ident"]
        wo = sb("wo", [P, DC, D])
        wr = sb("wr", [P, DC, NR])
        zero = sb("zero", [P, XW])
        mhalf = sb("mhalf", [P, 1])
        eps = sb("eps", [P, 1])
        fence = sb("fence", [P, 1])
        st = sb("st", [P, S, 6])
        mv = sb("mv", [P, S, 2])
        rs = sb("rs", [P, S, 2])
        XN = sb("XN", [P, S, D])
        XNT = sb("XNT", [P, DC, P])
        bo = sb("bo", [P, D])
        mask8 = sb("mask8", [1, BATCH * NCTX], mybir.dt.uint8)
        hide = sb("hide", [1, BATCH * NCTX])
        ones = sb("ones", [1, P])
        K = [sb(f"K{b}", [P, 2, KEYS0]) for b in range(2)]
        V = [sb(f"V{b}", [P, KC0, D]) for b in range(2)]
        Q = sb("Q", [P, S, H0, P])
        X = sb("X", [P, S, D])
        X1 = sb("X1", [P, S, D])
        E = sb("E", [P, 2, KEYS0])
        ET = sb("ET", [P, 2, KC0, P])
        O = sb("O", [P, 2, D])
        OT = sb("OT", [P, DC, P])
        pm = sb("pm", [P, HEADS, 3])
        nm = sb("nm", [P, HEADS])
        den = sb("den", [P, HEADS])
        rden = sb("rden", [P, HEADS])
        SC = [es.enter_context(nc.psum_tensor(f"s2_SC{k}", [P, 3 * 512], F32)) for k in range(2)]
        T = [es.enter_context(nc.psum_tensor(f"s2_T{k}", [P, 512], F32)) for k in range(2)]

        consts = sem("consts")
        setup = sem("setup")
        exponent = sem("exponent")
        kv_loaded = [sig(f"kv_loaded{b}", 2, 16, 0) for b in range(2)]
        q_loaded = [sig(f"q_loaded{s}", 2, 16) for s in range(S)]
        x_loaded = [sig(f"x_loaded{s}", 1, 16) for s in range(S)]
        s0_done = sig("s0_done", HEADS)
        s1_done = sig("s1_done", HEADS)
        s2_done = sig("s2_done", HEADS)
        nm_ready = sig("nm_ready", HEADS)
        exp_done = sig("exp_done", HEADS)
        turned = [sig(f"turned{g}", HEADS) for g in range(3)]
        et_ready = [sig(f"et_ready{g}", HEADS) for g in range(3)]
        av_done = sig("av_done", HEADS, 1, 2 * (TPB // S))
        o_ready = sig("o_ready", HEADS)
        o_turned = sig("o_turned", S)
        ot_ready = sig("ot_ready", S)
        y_done = sig("y_done", S)
        x1_ready = sig("x1_ready", S)
        stats = sig("stats", S)
        rstd = sig("rstd", S)
        xn_ready = sig("xn_ready", S)
        xn_turned = sig("xn_turned", S)
        xnt_ready = sig("xnt_ready", S)
        logits_done = sig("logits_done", S)
        logits_kept = sig("logits_kept", S)
        stored = [sig(f"stored{s}", 2, 16) for s in range(S)]
        cleared = sem("cleared")
        dve = Steps(sem("dve_steps"), 2 * HEADS + 2 * S)
        pool = Steps(sem("pool_steps"), S)
        PASSES = TPB // S

        def over_batches(eng, body):
            with eng.Fori(0, BATCH // 2) as bb:
                for half in range(2):
                    with eng.Fori(0, PASSES) as p:
                        body(half, bb * (2 * PASSES) + half * PASSES + p, bb, p)

        with nc.Block() as block:
            @block.sync
            def _(sp):
                sp.dma_start(wo[:], w["wo0"]).then_inc(consts, 16)
                sp.dma_start(bo[:], w["bo0"].partition_broadcast(P)).then_inc(consts, 16)
                sp.dma_start(wr[:], w["wr"]).then_inc(consts, 16)
                sp.dma_start(mask8[:], w["mask"]).then_inc(consts, 16)
                for s in range(S):
                    q_loaded[s].start(sp)
                    x_loaded[s].start(sp)
                    stored[s].start(sp)
                sp.wait_ge(setup, 4)
                rows = lambda i, s: bass.ds(i * (S * P) + s * P, P)

                def load_q(i, s):
                    for r in range(2):
                        sp.dma_start(Q[r * HD0:(r + 1) * HD0, s, r::2, :], scratch["q0"][bass.ds(i * S + s, 1), r * HD0:(r + 1) * HD0, :, :]
                                     .rearrange("a p c n -> (a p) c n")).then_inc(q_loaded[s].sem, 16)

                def load_x(i, s):
                    sp.dma_start(X[:, s, :], x[rows(i, s), :]).then_inc(x_loaded[s].sem, 16)

                def tiles(i, more):
                    for s in range(S):
                        if more:
                            sp.wait_ge(s2_done.sem, s2_done.now(i, s * H0 + H0 - 1))
                            load_q(i + 1, s)
                        sp.wait_ge(xn_ready.sem, xn_ready.now(i, s))
                        if more:
                            load_x(i + 1, s)
                        sp.dma_start(scratch["x1"][rows(i, s), :], X1[:, s, :]).then_inc(stored[s].sem, 16)
                        sp.dma_start(scratch["xn"][rows(i, s), :], XN[:, s, :]).then_inc(stored[s].sem, 16)

                for s in range(S):
                    load_q(0, s)
                    load_x(0, s)
                sp.dma_start(scratch["sorted"].rearrange("(p t) n -> p t n", p=P), zero[:].unsqueeze(1).to_broadcast([P, NTS, XW])).then_inc(cleared, 16)
                with sp.Fori(0, NT // S - 1) as i:
                    tiles(i, True)
                tiles(NT // S - 1, False)
                sp.wait_ge(cleared, 16)
                for s in range(S):
                    sp.wait_ge(stored[s].sem, stored[s].now(NT // S - 1, 1))

            @block.gpsimd
            def _(gp):
                
                def load(half, batch):
                    gp.dma_start(K[half][:], scratch["k0"][bass.ds(batch, 1), :, :, :].rearrange("a p c n -> (a p) c n")).then_inc(kv_loaded[half].sem, 16)
                    gp.dma_start(V[half][:], scratch["v0"][bass.ds(batch, 1), :, :, :].rearrange("a p c n -> (a p) c n")).then_inc(kv_loaded[half].sem, 16)

                rstd.start(gp)
                gp.memset(mhalf[:], -0.5).then_inc(exponent, 1)
                gp.memset(eps[:], EPS).then_inc(exponent, 1)
                gp.wait_ge(exponent, 2)
                load(0, 0)
                with gp.Fori(0, BATCH // 2) as bb:
                    for half in range(2):
                        if half == 0:
                            gp.wait_ge(av_done.sem, av_done.back(bb * (2 * PASSES) + PASSES - 1, HEADS - 1, PASSES))
                            load(1, bb * 2 + 1)
                        else:
                            gp.wait_ge(av_done.sem, av_done.back(bb * (2 * PASSES) + 2 * PASSES - 1, HEADS - 1, PASSES))
                            load(0, (bb * 2 + 2) % BATCH)
                        with gp.Fori(0, PASSES) as p:
                            i = bb * (2 * PASSES) + half * PASSES + p
                            for s in range(S):
                                gp.wait_ge(stats.sem, stats.now(i, s))
                                gp.tensor_tensor(rs[:, s, 0:1], mv[:, s, 1:2], eps[:], ALU.add).then_inc(*pool.mark())
                                gp.wait_ge(pool.sem, pool.last(i))
                                gp.tensor_tensor(rs[:, s, 1:2], rs[:, s, 0:1], mhalf[:], ALU.pow).then_inc(rstd.sem, 1)
                            pool.done()
                gp.wait_ge(kv_loaded[0].sem, kv_loaded[0].now(BATCH // 2, 1))

            @block.tensor
            def _(pe):
                for q in (s0_done, s1_done, s2_done, *turned, av_done, o_turned, y_done, xn_turned, logits_done):
                    q.start(pe)
                pe.wait_ge(consts, 64)
                pe.wait_ge(setup, 4)

                def body(half, i, bb, p):
                    Kb, Vb = K[half], V[half]
                    use = [0]

                    def bank():
                        use[0] += 1
                        return T[(use[0] - 1) % 2]

                    def q_of(j):
                        return Q[:, j // H0, j % H0, :], j % H0 // 2

                    def scores(j, part):
                        qt, ch = q_of(j)
                        out = SC[j % 2]
                        if part == 0 and j % H0 == 0:
                            pe.wait_ge(q_loaded[j // H0].sem, q_loaded[j // H0].now(i, 1))
                        if part < 2:
                            pe.matmul(out[:, part * 512:(part + 1) * 512], qt, Kb[:, ch, part * 512:(part + 1) * 512],
                                      start=True, stop=True).then_inc((s0_done, s1_done)[part].sem, 1)
                            return
                        if j >= 2:
                            pe.wait_ge(o_ready.sem, o_ready.now(i, j - 2))
                        else:
                            pe.wait_ge(o_ready.sem, o_ready.prev(i, HEADS - 2 + j))
                        pe.matmul(out[:, 1024:KEYS0], qt, Kb[:, ch, 1024:KEYS0], start=True, stop=False)
                        pe.matmul(out[:, 1024:KEYS0], ones[:], hide[0:1, bass.ds(bb * (2 * NCTX) + half * NCTX, NCTX)],
                                  start=False, stop=True).then_inc(s2_done.sem, 1)

                    def turn(j, g):
                        a, b = GROUPS[g]
                        if g == 0:
                            pe.wait_ge(exp_done.sem, exp_done.now(i, j))
                        if g == 2:
                            pe.wait_ge(et_ready[0].sem, et_ready[0].now(i, j))
                        t = bank()
                        for k in range(a, b):
                            n = min(P, KEYS0 - k * P)
                            ins = pe.transpose(t[0:n, (k - a) * P:(k - a + 1) * P], E[:, j % 2, k * P:k * P + n], ident[:])
                        ins.then_inc(turned[g].sem, 1)

                    def times_v(j, g):
                        a, b = GROUPS[g]
                        pe.wait_ge(et_ready[g].sem, et_ready[g].now(i, j))
                        for k in range(a, b):
                            n = min(P, KEYS0 - k * P)
                            ins = pe.matmul(SC[j % 2][:, 1280:1280 + P], ET[0:n, j % 2, k, :], Vb[0:n, k, (j % H0 // 2) * P:(j % H0 // 2 + 1) * P],
                                            start=(k == 0), stop=(k == KC0 - 1))
                        if g == 2:
                            ins.then_inc(av_done.sem, 1)

                    def turn_o(s, j):
                        pe.wait_ge(o_ready.sem, o_ready.now(i, s * H0 + H0 - 1))
                        pe.wait_ge(et_ready[1].sem, et_ready[1].now(i, j))
                        t = bank()
                        for k in range(DC):
                            ins = pe.transpose(t[:, k * P:(k + 1) * P], O[:, s % 2, k * P:(k + 1) * P], ident[:])
                        ins.then_inc(o_turned.sem, 1)

                    def project(s, j):
                        pe.wait_ge(ot_ready.sem, ot_ready.now(i, s))
                        pe.wait_ge(et_ready[2].sem, et_ready[2].now(i, j))
                        t = bank()
                        for k in range(DC):
                            ins = pe.matmul(t[:, 0:D], OT[:, k, :], wo[:, k, :], start=(k == 0), stop=(k == DC - 1))
                        ins.then_inc(y_done.sem, 1)

                    def turn_xn(s, j):
                        pe.wait_ge(xn_ready.sem, xn_ready.now(i, s))
                        pe.wait_ge(et_ready[1].sem, et_ready[1].now(i, j))
                        t = bank()
                        for k in range(DC):
                            ins = pe.transpose(t[:, k * P:(k + 1) * P], XN[:, s, k * P:(k + 1) * P], ident[:])
                        ins.then_inc(xn_turned.sem, 1)

                    def route(s, j):
                        pe.wait_ge(xnt_ready.sem, xnt_ready.now(i, s))
                        pe.wait_ge(et_ready[1].sem, et_ready[1].now(i, j))
                        t = bank()
                        for k in range(DC):
                            ins = pe.matmul(t[:, 0:NR], XNT[:, k, :], wr[:, k, :], start=(k == 0), stop=(k == DC - 1))
                        ins.then_inc(logits_done.sem, 1)

                    pe.wait_ge(kv_loaded[half].sem, kv_loaded[half].now(bb, 1))
                    for part in range(3):
                        scores(0, part)
                    for j in range(HEADS):
                        more = j + 1 < HEADS
                        done = j // H0 - 1 if j and j % H0 == 0 else None
                        if more:
                            scores(j + 1, 0)
                        turn(j, 0)
                        if more:
                            scores(j + 1, 1)
                        if j % H0 == 1 and j > 1:
                            pe.wait_ge(x1_ready.sem, x1_ready.now(i, j // H0 - 1))
                        elif j % H0 == 2 and j > 2:
                            pe.wait_ge(xnt_ready.sem, xnt_ready.now(i, j // H0 - 1))
                        elif j % H0 == 3 and j > 3:
                            pe.wait_ge(logits_kept.sem, logits_kept.now(i, j // H0 - 1))
                        elif j == 0:
                            pe.wait_ge(logits_kept.sem, logits_kept.prev(i, S - 1))
                        turn(j, 1)
                        if more:
                            scores(j + 1, 2)
                        turn(j, 2)
                        if done is not None:
                            turn_o(done, j)
                        times_v(j, 0)
                        times_v(j, 1)
                        if done is not None:
                            project(done, j)
                        times_v(j, 2)
                        if j > H0 and j % H0 == 1:
                            turn_xn(j // H0 - 1, j)
                        if j > H0 and j % H0 == 2:
                            route(j // H0 - 1, j)
                    turn_o(S - 1, HEADS - 1)
                    project(S - 1, HEADS - 1)
                    turn_xn(S - 1, HEADS - 1)
                    route(S - 1, HEADS - 1)
                    assert use[0] % 2 == 0

                over_batches(pe, body)

            @block.scalar
            def _(a):
                a.wait_ge(kv_loaded[0].sem, kv_loaded[0].now(0, 1))
                a.wait_ge(x_loaded[S - 1].sem, x_loaded[S - 1].now(0, 0))
                for n in range(EXPERTS):
                    part = slice(n * 2 * DC, (n + 1) * 2 * DC)
                    a.dma_start(c["gate_up"][:, part, :], w["gate_up"][:, part, :]).then_inc(c["experts_loaded"], 16)
                for q in (exp_done, et_ready[1], ot_ready, xnt_ready):
                    q.start(a)

                def body(half, i, bb, p):
                    use = [0]

                    def exp(j):
                        a.wait_ge(nm_ready.sem, nm_ready.now(i, j))
                        a.activation(E[:, j % 2, :], SC[j % 2][:, 0:KEYS0], ACT.Exp, bias=nm[:, j:j + 1],
                                     accum_out=den[:, j:j + 1]).then_inc(exp_done.sem, 1)

                    exp(0)
                    for j in range(HEADS):
                        a.wait_ge(turned[1].sem, turned[1].now(i, j))
                        use[0] += 3
                        a.copy(ET[:, j % 2, 4:8, :].rearrange("p a b -> p (a b)"), T[(use[0] - 2) % 2][:]).then_inc(et_ready[1].sem, 1)
                        tiles = ([j // H0 - 1] if j and j % H0 == 0 else []) + ([S - 1] if j == HEADS - 1 else [])
                        for s in tiles:
                            a.wait_ge(o_turned.sem, o_turned.now(i, s))
                            use[0] += 2
                            a.copy(OT[:].rearrange("p a b -> p (a b)"), T[(use[0] - 2) % 2][:, 0:D]).then_inc(ot_ready.sem, 1)
                        if j + 1 < HEADS:
                            exp(j + 1)
                        for s in ([j // H0 - 1] if j > H0 and j % H0 == 1 else []) + ([S - 1] if j == HEADS - 1 else []):
                            a.wait_ge(xn_turned.sem, xn_turned.now(i, s))
                            use[0] += 1
                            a.copy(XNT[:].rearrange("p a b -> p (a b)"), T[(use[0] - 1) % 2][:, 0:D]).then_inc(xnt_ready.sem, 1)
                        if j > H0 and j % H0 == 2:
                            use[0] += 1

                over_batches(a, body)

            @block.vector
            def _(v):
                for q in (nm_ready, et_ready[0], et_ready[2], o_ready, x1_ready, stats, xn_ready, logits_kept):
                    q.start(v)
                v.memset(zero[:], 0.0)
                v.memset(Q[:], 0.0).then_inc(setup, 1)
                v.memset(ones[:], 1.0).then_inc(setup, 1)
                v.wait_ge(consts, 64)
                v.tensor_copy(hide[:], mask8[:]).then_inc(setup, 1)
                v.wait_ge(setup, 3)
                v.tensor_scalar(hide[:], hide[:], -1.0, BIG, ALU.add, ALU.mult).then_inc(setup, 1)

                def body(half, i, bb, p):
                    use = [0]

                    def part_max(j, part):
                        q = (s0_done, s1_done, s2_done)[part]
                        v.wait_ge(q.sem, q.now(i, j))
                        ins = v.tensor_reduce(pm[:, j, part:part + 1], SC[j % 2][:, part * 512:min(part * 512 + 512, KEYS0)], AX_X, ALU.max)
                        if part == 2:
                            ins.then_inc(*dve.mark())
                            v.wait_ge(dve.sem, dve.last(i))
                            v.tensor_reduce(nm[:, j:j + 1], pm[:, j, :], AX_X, ALU.max, negate=True).then_inc(nm_ready.sem, 1)

                    def evac(j, g):
                        a, b = GROUPS[g]
                        v.wait_ge(turned[g].sem, turned[g].now(i, j))
                        t = T[(use[0] + (0, None, 0)[g]) % 2]
                        if g == 0:
                            v.tensor_copy(ET[:, j % 2, a:b, :].rearrange("p a b -> p (a b)"), t[:]).then_inc(et_ready[0].sem, 1)
                            return
                        v.tensor_copy(ET[:, j % 2, a, :], t[:, 0:P])
                        v.tensor_copy(ET[0:TAIL, j % 2, a + 1, :], t[0:TAIL, P:2 * P]).then_inc(et_ready[2].sem, 1)

                    def head_out(j):
                        v.wait_ge(exp_done.sem, exp_done.now(i, j))
                        v.reciprocal(rden[:, j:j + 1], den[:, j:j + 1]).then_inc(*dve.mark())
                        v.wait_ge(dve.sem, dve.last(i))
                        v.wait_ge(av_done.sem, av_done.now(i, j))
                        if j % H0 == 0:
                            s = j // H0
                            q = o_turned.now(i, s - 2) if s >= 2 else o_turned.prev(i, S - 2 + s)
                            v.wait_ge(o_turned.sem, q)
                        h = j % H0
                        v.tensor_scalar(O[:, j // H0 % 2, h * HD0:(h + 1) * HD0], SC[j % 2][:, 1280 + h % 2 * HD0:1280 + (h % 2 + 1) * HD0], rden[:, j:j + 1], None,
                                        ALU.mult).then_inc(o_ready.sem, 1)

                    def tile_out(s):
                        v.wait_ge(x_loaded[s].sem, x_loaded[s].now(i, 0))
                        v.tensor_tensor(X[:, s, :], X[:, s, :], bo[:], ALU.add).then_inc(*dve.mark())
                        v.wait_ge(dve.sem, dve.last(i))
                        v.wait_ge(stored[s].sem, stored[s].prev(i, 1))
                        v.wait_ge(y_done.sem, y_done.now(i, s))
                        v.tensor_tensor(X1[:, s, :], T[(use[0] - 1) % 2][:, 0:D], X[:, s, :], ALU.add).then_inc(x1_ready.sem, 1)
                        v.wait_ge(x1_ready.sem, x1_ready.now(i, s))
                        v.bn_stats(st[:, s, :], X1[:, s, :]).then_inc(*dve.mark())
                        v.wait_ge(dve.sem, dve.last(i))
                        v.memset(fence[:], 0.0)
                        v.bn_aggr(mv[:, s, :], st[:, s, :]).then_inc(stats.sem, 1)

                    def tile_norm(s):
                        v.wait_ge(rstd.sem, rstd.now(i, s))
                        v.tensor_scalar(XN[:, s, :], X1[:, s, :], mv[:, s, 0:1], rs[:, s, 1:2], ALU.subtract, ALU.mult).then_inc(xn_ready.sem, 1)
                        use[0] += 1

                    def tile_logits(s):
                        v.wait_ge(logits_done.sem, logits_done.now(i, s))
                        use[0] += 1
                        v.tensor_scalar(c["logits"][:, bass.ds(i * S + s, 1), :].rearrange("p a n -> p (a n)"), T[(use[0] - 1) % 2][:, 0:NR],
                                        1.0, None, ALU.mult).then_inc(logits_kept.sem, 1)

                    for part in range(3):
                        part_max(0, part)
                    for j in range(HEADS):
                        more = j + 1 < HEADS
                        if more:
                            part_max(j + 1, 0)
                        evac(j, 0)
                        if more:
                            part_max(j + 1, 1)
                            part_max(j + 1, 2)
                        evac(j, 2)
                        use[0] += 3
                        if j and j % H0 == 0:
                            use[0] += 2
                            tile_out(j // H0 - 1)
                        if j > H0 and j % H0 == 1:
                            tile_norm(j // H0 - 1)
                        head_out(j)
                        if j > H0 and j % H0 == 2:
                            tile_logits(j // H0 - 1)
                    use[0] += 2
                    tile_out(S - 1)
                    tile_norm(S - 1)
                    tile_logits(S - 1)
                    dve.done()

                over_batches(v, body)
    sems.release()


def route_tokens(nc, c, w, scratch):
    G = MGROUPS
    R = 16
    sems = Semaphores(nc)
    with ExitStack() as es:
        def sb(name, shape, dt=F32):
            return es.enter_context(nc.sbuf_tensor("s3_" + name, shape, dt))

        def sem(name):
            return sems.take("s3_" + name)

        LG, WT, POS, GRP = c["logits"], c["weights"], c["rows"], c["group"]
        before = sb("before", [P, P])
        ones = sb("ones", [P, P])
        starts = sb("starts", [P, NTS])
        sg = sb("sg", [P, NT, NR])
        best = sb("best", [P, NT])
        eq = sb("eq", [P, NT, G])
        anyb = sb("anyb", [P, NT, 1])
        hot = sb("hot", [P, NT, G])
        mval = sb("mval", [P, NT])
        tmp = sb("tmp", [P, NT])
        pick = sb("pick", [P, NT, G, 2])
        sel = sb("sel", [P, NT, 2])
        runs = [sb(f"runs{k}", [P, NT, G]) for k in range(2)]
        total = sb("total", [P, NT, G])
        sizes = sb("sizes", [P, G])
        isizes = sb("isizes", [P, G], I32)
        base = sb("base", [P, G])
        place = sb("place", [P, NT, G])
        steps = sb("steps", [P, NTS])
        B = sb("B", [P, R, XW])
        IX = sb("IX", [P, R], I32)
        RK = [es.enter_context(nc.psum_tensor(f"s3_R{k}", [P, NT * G], F32)) for k in range(2)]

        consts = sem("consts")
        negexp = sem("negexp")
        dve = sem("dve_steps")
        hot_ready = sem("hot_ready")
        counted = sem("counted")
        taken = sem("taken")
        routed = sem("routed")
        loaded = [Signal(sem(f"loaded{s}"), 1, 16) for s in range(R)]
        row_ready = Signal(sem("row_ready"), R)
        scattered = [Signal(sem(f"scattered{s}"), 1, 16, 0) for s in range(R)]
        freed = [Signal(sem(f"freed{s}"), 1) for s in range(R)]

        with nc.Block() as block:
            @block.sync
            def _(sp):
                sp.dma_start(before[:], w["before"]).then_inc(consts, 16)
                sp.dma_start(starts[:], w["starts"].partition_broadcast(P)).then_inc(consts, 16)
                for s in range(R):
                    loaded[s].start(sp)
                with sp.Fori(0, NT // R) as i:
                    for s in range(R):
                        sp.wait_ge(freed[s].sem, freed[s].prev(i, 0))
                        sp.dma_start(B[:, s, 0:D], scratch["xn"][bass.ds(i * (R * P) + s * P, P), :]).then_inc(loaded[s].sem, 16)

            @block.gpsimd
            def _(gp):
                for s in range(R):
                    freed[s].start(gp)
                with gp.Fori(0, NT // R) as i:
                    for s in range(R):
                        gp.wait_ge(row_ready.sem, row_ready.now(i, s))
                        gp.sem_inc(taken, 1)
                        gp.indirect_dma_start(scratch["sorted"], bass.IndirectOffsetOnAxis(ap=IX[:, s:s + 1], axis=0),
                                              B[:, s, :], None).then_inc(scattered[s].sem, 16)
                    for s in range(R):
                        gp.wait_ge(scattered[s].sem, scattered[s].now(i, 0))
                        gp.sem_inc(freed[s].sem, 1)

            @block.tensor
            def _(pe):
                pe.wait_ge(consts, 32)
                pe.wait_ge(hot_ready, 1)
                flat = hot[:].rearrange("p t g -> p (t g)")
                pe.matmul(RK[0][:], before[:], flat, start=True, stop=True)
                pe.matmul(RK[1][:], ones[:], flat, start=True, stop=True).then_inc(counted, 1)

            @block.scalar
            def _(a):
                for n in range(MGROUPS):
                    part = slice(n * 2 * FFN // P, (n + 1) * 2 * FFN // P)
                    a.dma_start(c["down"][:, part, :], w["down"][:, part, :]).then_inc(c["experts_loaded"], 16)
                a.activation(sg[:].rearrange("p t n -> p (t n)"), LG[:].rearrange("p t n -> p (t n)"), ACT.Exp, scale=-1.0).then_inc(negexp, 1)

            @block.vector
            def _(v):
                at = [0]

                def step(ins):
                    at[0] += 1
                    ins.then_inc(dve, 1)
                    v.wait_ge(dve, at[0])

                v.memset(ones[:], 1.0)
                row_ready.start(v)
                v.wait_ge(negexp, 1)
                flat = sg[:].rearrange("p t n -> p (t n)")
                step(v.tensor_scalar(flat, flat, 1.0, None, ALU.add))
                step(v.reciprocal(flat, flat))
                step(v.tensor_reduce(best[:], sg[:, :, 0:G], AX_X, ALU.max))
                step(v.tensor_tensor(eq[:], sg[:, :, 0:G], best[:].unsqueeze(2).to_broadcast([P, NT, G]), ALU.is_equal))
                step(v.tensor_copy(hot[:, :, 0:1], eq[:, :, 0:1]))
                step(v.tensor_copy(anyb[:], eq[:, :, 0:1]))
                for g in range(1, G):
                    step(v.tensor_tensor(hot[:, :, g:g + 1], eq[:, :, g:g + 1], anyb[:], ALU.is_gt))
                    step(v.tensor_tensor(anyb[:], anyb[:], eq[:, :, g:g + 1], ALU.max))
                v.sem_inc(hot_ready, 1)
                step(v.tensor_scalar(tmp[:], best[:], 1e-9, None, ALU.add))
                step(v.reciprocal(tmp[:], tmp[:]))
                step(v.tensor_tensor(mval[:], best[:], tmp[:], ALU.mult))
                step(v.tensor_tensor(pick[:], sg[:, :, G:NR].rearrange("p t (g e) -> p t g e", e=2),
                                     hot[:].unsqueeze(3).to_broadcast([P, NT, G, 2]), ALU.mult))
                step(v.tensor_reduce(sel[:], pick[:].rearrange("p t g e -> p t e g"), AX_X, ALU.add))
                step(v.tensor_reduce(tmp[:], sel[:], AX_X, ALU.add))
                step(v.tensor_scalar(tmp[:], tmp[:], 1e-9, None, ALU.add))
                step(v.reciprocal(tmp[:], tmp[:]))
                step(v.tensor_tensor(tmp[:], tmp[:], mval[:], ALU.mult))
                step(v.tensor_tensor(WT[:], sel[:], tmp[:].unsqueeze(2).to_broadcast([P, NT, 2]), ALU.mult))
                v.wait_ge(counted, 1)
                three = lambda r: r[:].rearrange("p (t g) -> p t g", g=G)
                step(v.tensor_copy(total[:], three(RK[1])))
                step(v.tensor_copy(runs[0][:], total[:]))
                k, d = 0, 1
                while d < NT:
                    a, b = runs[k], runs[1 - k]
                    step(v.tensor_copy(b[:, 0:d, :], a[:, 0:d, :]))
                    step(v.tensor_tensor(b[:, d:NT, :], a[:, d:NT, :], a[:, 0:NT - d, :], ALU.add))
                    k, d = 1 - k, 2 * d
                run = runs[k]
                step(v.tensor_scalar(sizes[:], run[:, NT - 1, :], float(P - 1), None, ALU.add))
                step(v.tensor_copy(isizes[:], sizes[:]))
                step(v.tensor_scalar(isizes[:], isizes[:], -P, None, ALU.bitwise_and))
                step(v.tensor_copy(sizes[:], isizes[:]))
                step(v.memset(base[:], 0.0))
                for g in range(1, G):
                    step(v.tensor_tensor(base[:, g:g + 1], base[:, g - 1:g], sizes[:, g - 1:g], ALU.add))
                step(v.tensor_tensor(place[:], run[:], total[:], ALU.subtract))
                step(v.tensor_tensor(place[:], place[:], three(RK[0]), ALU.add))
                step(v.tensor_tensor(place[:], place[:], base[:].unsqueeze(1).to_broadcast([P, NT, G]), ALU.add))
                step(v.tensor_tensor(place[:], place[:], hot[:], ALU.mult))
                step(v.tensor_reduce(POS[:, 0:NT], place[:], AX_X, ALU.add))
                step(v.tensor_copy(POS[:, NT:NT + TPB], POS[:, 0:TPB]))
                v.wait_ge(consts, 32)
                step(v.tensor_scalar(steps[:], starts[:], base[:, 1:2], None, ALU.is_ge))
                for g in range(2, G):
                    step(v.scalar_tensor_tensor(steps[:], starts[:], base[:, g:g + 1], steps[:], ALU.is_ge, ALU.add))
                step(v.tensor_copy(GRP[:], steps[:]))
                with v.Fori(0, NT // R) as i:
                    for s in range(R):
                        v.wait_ge(loaded[s].sem, loaded[s].now(i, 0))
                        v.tensor_scalar(B[:, s, D:XW], WT[:, bass.ds(i * R + s, 1), :].rearrange("p a n -> p (a n)"), 1.0, None, ALU.mult)
                        v.tensor_scalar(IX[:, s:s + 1], POS[:, bass.ds(i * R + s, 1)], 1.0, None, ALU.mult).then_inc(row_ready.sem, 1)
    sems.release()


def experts(nc, c, w, scratch):
    U = 2 * S
    FC = FFN // P
    sems = Semaphores(nc)
    with ExitStack() as es:
        def sb(name, shape, dt=F32):
            return es.enter_context(nc.sbuf_tensor("s4_" + name, shape, dt))

        def sem(name):
            return sems.take("s4_" + name)

        def sig(name, per, unit=1, ahead=1):
            return Signal(sem(name), per, unit, ahead)

        ident, GRP = c["ident"], c["group"]
        GU, DN = c["gate_up"], c["down"]
        X = sb("X", [P, S, XW])
        XT = sb("XT", [P, 2, DC, P])
        SG = sb("SG", [P, 2, FFN])
        H = sb("H", [P, 2, FFN])
        HT = sb("HT", [P, 2, FC, P])
        Y = sb("Y", [P, S, D])
        A = [es.enter_context(nc.psum_tensor(f"s4_A{k}", [P, 2, FFN], F32)) for k in range(2)]
        T = [es.enter_context(nc.psum_tensor(f"s4_T{k}", [P, 512], F32)) for k in range(2)]
        O = [es.enter_context(nc.psum_tensor(f"s4_O{k}", [P, 512], F32)) for k in range(2)]

        loaded = [sig(f"loaded{s}", 1, 16) for s in range(S)]
        x_turned = sig("x_turned", S)
        xt_ready = sig("xt_ready", S)
        gu_done = sig("gu_done", U)
        silu_done = sig("silu_done", U)
        h_ready = sig("h_ready", U)
        h_turned = sig("h_turned", U)
        ht_ready = sig("ht_ready", U)
        down_done = sig("down_done", S)
        y_ready = sig("y_ready", S)
        stored = [sig(f"stored{s}", 1, 16) for s in range(S)]
        NP = NTS // S

        with nc.Block() as block:
            @block.sync
            def _(sp):
                for s in range(S):
                    loaded[s].start(sp)
                    stored[s].start(sp)
                rows = lambda i, s: bass.ds(i * (S * P) + s * P, P)

                def load(i, s):
                    sp.dma_start(X[:, s, :], scratch["sorted"][rows(i, s), :]).then_inc(loaded[s].sem, 16)

                def tiles(i, more):
                    for s in range(S):
                        if more:
                            sp.wait_ge(h_ready.sem, h_ready.now(i, 2 * s + 1))
                            load(i + 1, s)
                        sp.wait_ge(y_ready.sem, y_ready.now(i, s))
                        sp.dma_start(scratch["ys"][rows(i, s), :], Y[:, s, :]).then_inc(stored[s].sem, 16)

                for s in range(S):
                    load(0, s)
                with sp.Fori(0, NP - 1) as i:
                    tiles(i, True)
                tiles(NP - 1, False)
                for s in range(S):
                    sp.wait_ge(stored[s].sem, stored[s].now(NP - 1, 0))

            @block.tensor
            def _(pe):
                for q in (x_turned, gu_done, h_turned, down_done):
                    q.start(pe)
                pe.wait_ge(c["experts_loaded"], 16 * (EXPERTS + MGROUPS))
                with pe.Fori(0, NP) as i:
                    groups = [None] * S

                    def turn_x(s):
                        pe.wait_ge(loaded[s].sem, loaded[s].now(i, 0))
                        if s < 2:
                            pe.wait_ge(y_ready.sem, y_ready.prev(i, S - 2 + s))
                        else:
                            pe.wait_ge(y_ready.sem, y_ready.now(i, s - 2))
                        for k in range(DC):
                            ins = pe.transpose(O[s % 2][:, k * P:(k + 1) * P], X[:, s, k * P:(k + 1) * P], ident[:])
                        ins.then_inc(x_turned.sem, 1)
                        groups[s] = pe.value_load(GRP[0:1, bass.ds(i * S + s, 1)], min_val=0, max_val=MGROUPS - 1)

                    def gate_up(u):
                        s, e = u // 2, u % 2
                        if e == 0:
                            pe.wait_ge(xt_ready.sem, xt_ready.now(i, s))
                        if u < 2:
                            pe.wait_ge(h_ready.sem, h_ready.prev(i, U - 2 + u))
                        else:
                            pe.wait_ge(h_ready.sem, h_ready.now(i, u - 2))
                        for k in range(DC):
                            for n in range(2):
                                ins = pe.matmul(A[u % 2][:, n, :], XT[:, s % 2, k, :],
                                                GU[:, bass.ds(groups[s] * (2 * DC * 2) + (e * DC + k) * 2 + n, 1), :].rearrange("p a n -> p (a n)"),
                                                start=(k == 0), stop=(k == DC - 1), skip_group_check=True)
                        ins.then_inc(gu_done.sem, 1)

                    def turn_h(u):
                        pe.wait_ge(h_ready.sem, h_ready.now(i, u))
                        if u < 2:
                            pe.wait_ge(ht_ready.sem, ht_ready.prev(i, U - 2 + u))
                        else:
                            pe.wait_ge(ht_ready.sem, ht_ready.now(i, u - 2))
                        for k in range(FC):
                            ins = pe.transpose(T[u % 2][:, k * P:(k + 1) * P], H[:, u % 2, k * P:(k + 1) * P], ident[:])
                        ins.then_inc(h_turned.sem, 1)

                    def down(u):
                        s, e = u // 2, u % 2
                        pe.wait_ge(ht_ready.sem, ht_ready.now(i, u))
                        for k in range(FC):
                            ins = pe.matmul(O[s % 2][:, D:2 * D], HT[:, u % 2, k, :],
                                            DN[:, bass.ds(groups[s] * (2 * FC) + e * FC + k, 1), :].rearrange("p a n -> p (a n)"),
                                            start=(e == 0 and k == 0), stop=(e == 1 and k == FC - 1), skip_group_check=True)
                        if e == 1:
                            ins.then_inc(down_done.sem, 1)

                    turn_x(0)
                    gate_up(0)
                    turn_x(1)
                    for u in range(U):
                        if u + 1 < U:
                            gate_up(u + 1)
                        turn_h(u)
                        if u:
                            down(u - 1)
                        if u % 2 == 0 and u >= 2 and u // 2 + 1 < S:
                            turn_x(u // 2 + 1)
                    down(U - 1)

            @block.scalar
            def _(a):
                for q in (silu_done, xt_ready):
                    q.start(a)
                with a.Fori(0, NP) as i:
                    def x_out(s):
                        a.wait_ge(x_turned.sem, x_turned.now(i, s))
                        a.copy(XT[:, s % 2, :, :].rearrange("p a b -> p (a b)"), O[s % 2][:, 0:D]).then_inc(xt_ready.sem, 1)

                    x_out(0)
                    x_out(1)
                    for u in range(U):
                        a.wait_ge(gu_done.sem, gu_done.now(i, u))
                        a.activation(SG[:, u % 2, :], A[u % 2][:, 0, :], ACT.Silu).then_inc(silu_done.sem, 1)
                        if u % 2 == 0 and u >= 2 and u // 2 + 1 < S:
                            x_out(u // 2 + 1)

            @block.vector
            def _(v):
                for q in (h_ready, ht_ready, y_ready):
                    q.start(v)
                with v.Fori(0, NP) as i:
                    def ht_out(u):
                        v.wait_ge(h_turned.sem, h_turned.now(i, u))
                        v.tensor_copy(HT[:, u % 2, :, :].rearrange("p a b -> p (a b)"), T[u % 2][:]).then_inc(ht_ready.sem, 1)

                    def y_out(s):
                        v.wait_ge(down_done.sem, down_done.now(i, s))
                        v.wait_ge(stored[s].sem, stored[s].prev(i, 0))
                        v.tensor_copy(Y[:, s, :], O[s % 2][:, D:2 * D]).then_inc(y_ready.sem, 1)

                    for u in range(U):
                        s, e = u // 2, u % 2
                        v.wait_ge(silu_done.sem, silu_done.now(i, u))
                        v.scalar_tensor_tensor(H[:, u % 2, :], SG[:, u % 2, :], X[:, s, D + e:D + e + 1], A[u % 2][:, 1, :],
                                               ALU.mult, ALU.mult).then_inc(h_ready.sem, 1)
                        ht_out(u)
                        if u % 2 == 0 and u >= 2:
                            y_out(u // 2 - 1)
                    y_out(S - 1)
    sems.release()


def attention1(nc, c, w, scratch):
    N = TPB
    HU = 4
    UT = H1 // HU
    U = N * UT
    VW = 6 * V1W
    sems = Semaphores(nc)
    with ExitStack() as es:
        def sb(name, shape, dt=F32):
            return es.enter_context(nc.sbuf_tensor("s5_" + name, shape, dt))

        def sem(name):
            return sems.take("s5_" + name)

        def sig(name, per, unit=1, ahead=1):
            return Signal(sem(name), per, unit, ahead)

        ident, POS = c["ident"], c["rows"]
        wq = sb("wq", [P, DC, D])
        wo = sb("wo", [P, DC, D])
        bo = sb("bo", [P, D])
        cols = sb("cols", [P, DC + 1 + P // HD1])
        bq, scale, own = cols[:, 0:DC], cols[:, DC:DC + 1], cols[:, DC + 1:]
        mhalf = sb("mhalf", [P, 1])
        eps = sb("eps", [P, 1])
        fence = sb("fence", [P, 1])
        K1 = sb("K1", [P, DC, NCTX])
        KB = sb("KB", [P, DC, P // HD1, NCTX])
        VM = sb("VM", [P, V1 + VW - V1W])
        VT = sb("VT", [P, V1])
        XA = sb("XA", [P, 4, D])
        G = sb("G", [P, 4, D])
        IX = sb("IX", [P, 4], I32)
        X2 = sb("X2", [P, 4, D])
        XB = sb("XB", [P, 4, D])
        st = sb("st", [P, 4, 6])
        mv = sb("mv", [P, 4, 2])
        rs = sb("rs", [P, 4, 2])
        XN = sb("XN", [P, 2, D])
        XNT = sb("XNT", [P, DC, P])
        QT = sb("QT", [P, 2, DC, P])
        mx = sb("mx", [P, 2, HU])
        SB = sb("SB", [P, 2, HU, NCTX])
        E = sb("E", [P, 2, HU, P])
        EP = sb("EP", [P, 2, HU, TPAD])
        EM = sb("EM", [P, 2, HU, P])
        EL = sb("EL", [P, 2, P])
        rden = sb("rden", [P, 2, HU, 1])
        O = sb("O", [P, 2, D])
        OT = sb("OT", [P, DC, P])
        X3 = sb("X3", [P, 4, D])
        SC = [es.enter_context(nc.psum_tensor(f"s5_SC{k}", [P, 2, 512], F32)) for k in range(2)]
        T = [es.enter_context(nc.psum_tensor(f"s5_T{k}", [P, 512], F32)) for k in range(2)]
        OB = [es.enter_context(nc.psum_tensor(f"s5_OB{k}", [P, 512], F32)) for k in range(2)]

        consts = sem("consts")
        setup = sem("setup")
        k_loaded = sig("k_loaded", 1, 16)
        v_loaded = sig("v_loaded", 2, 16)
        x_loaded = [sig(f"x_loaded{s}", 2, 16) for s in range(4)]
        g_loaded = [sig(f"g_loaded{s}", 2, 16, 0) for s in range(4)]
        ix_ready = sig("ix_ready", N)
        kb_ready = sig("kb_ready", 1)
        x2_ready = sig("x2_ready", N)
        stats = sig("stats", N)
        rstd = sig("rstd", N)
        xn_ready = sig("xn_ready", N)
        xn_turned = sig("xn_turned", N)
        xnt_ready = sig("xnt_ready", N)
        q_done = sig("q_done", N)
        qt_ready = sig("qt_ready", N)
        scored = sig("scored", U)
        lowered = sig("lowered", U)
        exp_done = sig("exp_done", U)
        main_turned = sig("main_turned", U)
        main_kept = sig("main_kept", U)
        tail_turned = sig("tail_turned", U)
        tail_kept = sig("tail_kept", U)
        av_done = sig("av_done", U)
        o_ready = sig("o_ready", U)
        o_turned = sig("o_turned", N)
        ot_ready = sig("ot_ready", N)
        y_done = sig("y_done", N)
        x3_ready = sig("x3_ready", N)
        stored = [sig(f"stored{s}", 2, 16) for s in range(4)]
        NCONST = 4
        dve = Steps(sem("dve_steps"), N + U + U)
        dve0 = sem("dve_first_steps")
        pool = Steps(sem("pool_steps"), N)

        with nc.Block() as block:
            @block.sync
            def _(sp):
                for dst, src in ((wq, w["wq1"]), (wo, w["wo1"]), (cols, w["cols1"])):
                    sp.dma_start(dst[:], src).then_inc(consts, 16)
                sp.dma_start(bo[:], w["bo1"].partition_broadcast(P)).then_inc(consts, 16)
                k_loaded.start(sp)
                v_loaded.start(sp)
                for s in range(4):
                    x_loaded[s].start(sp)
                    stored[s].start(sp)

                def load_x(tile, s):
                    sp.dma_start(XA[:, s, :], scratch["x1"][bass.ds(tile * P, P), :]).then_inc(x_loaded[s].sem, 16)

                sp.wait_ge(setup, 4)
                for s in range(4):
                    load_x(s, s)
                with sp.Fori(0, BATCH) as b:
                    sp.wait_ge(kb_ready.sem, kb_ready.prev(b, 0))
                    sp.dma_start(K1[:], scratch["k1"][bass.ds(b, 1), :, :, :].rearrange("a p c n -> (a p) c n")).then_inc(k_loaded.sem, 16)
                    sp.wait_ge(av_done.sem, av_done.prev(b, U - 1))
                    for k, dst in enumerate((VM[:, 0:V1], VT[:])):
                        sp.dma_start(dst, scratch["v1"][bass.ds(b, 1), :, k:k + 1, :].rearrange("a p c n -> (a p) (c n)")).then_inc(v_loaded.sem, 16)
                    for n in range(N):
                        sp.wait_ge(x2_ready.sem, x2_ready.now(b, n))
                        load_x(b * N + n + 4 if n < 4 else ((b + 1) % BATCH) * N + n - 4, n % 4)
                        sp.wait_ge(x3_ready.sem, x3_ready.now(b, n))
                        sp.dma_start(scratch["x3"][bass.ds(b * SEQ + n * P, P), :],
                                     X3[:, n % 4, :]).then_inc(stored[n % 4].sem, 16)
                for s in range(4):
                    sp.wait_ge(stored[s].sem, stored[s].now(BATCH - 1, 1))
                    sp.wait_ge(x_loaded[s].sem, x_loaded[s].now(BATCH, 0))

            @block.gpsimd
            def _(gp):
                rstd.start(gp)
                gp.memset(mhalf[:], -0.5).then_inc(setup, 1)
                gp.memset(eps[:], EPS).then_inc(setup, 1)
                gp.wait_ge(setup, 4)

                def gather(s):
                    gp.indirect_dma_start(G[:, s, :], None, scratch["ys"], bass.IndirectOffsetOnAxis(ap=IX[:, s:s + 1], axis=0)).then_inc(g_loaded[s].sem, 16)

                def scale_of(b, n, first=False):
                    s = n % 4
                    gp.wait_ge(stats.sem, stats.now(b, n))
                    if first:
                        gp.tensor_tensor(rs[:, s, 0:1], mv[:, s, 1:2], eps[:], ALU.add).then_inc(setup, 1)
                        gp.wait_ge(setup, 5 + n)
                    else:
                        gp.tensor_tensor(rs[:, s, 0:1], mv[:, s, 1:2], eps[:], ALU.add).then_inc(*pool.mark())
                        gp.wait_ge(pool.sem, pool.last(b))
                    gp.tensor_tensor(rs[:, s, 1:2], rs[:, s, 0:1], mhalf[:], ALU.pow).then_inc(rstd.sem, 1)

                for s in range(4):
                    gp.wait_ge(ix_ready.sem, ix_ready.now(0, s))
                    gather(s)
                for n in range(2):
                    scale_of(0, n, True)
                with gp.Fori(0, BATCH) as b:
                    for n in range(N):
                        gp.wait_ge(ix_ready.sem, ix_ready.now(b, n + 4))
                        scale_of(b, n + 2)
                        gather(n % 4)
                    pool.done()
                for s in range(4):
                    gp.wait_ge(g_loaded[s].sem, g_loaded[s].now(BATCH, 0))

            @block.tensor
            def _(pe):
                for q in (xn_turned, q_done, scored, main_turned, tail_turned, av_done, o_turned, y_done):
                    q.start(pe)
                pe.wait_ge(consts, 16 * NCONST)

                def turn_xn(b, n):
                    pe.wait_ge(xn_ready.sem, xn_ready.now(b, n))
                    for k in range(DC):
                        ins = pe.transpose(T[0][:, k * P:(k + 1) * P], XN[:, n % 2, k * P:(k + 1) * P], ident[:])
                    ins.then_inc(xn_turned.sem, 1)

                def queries(b, n):
                    pe.wait_ge(xnt_ready.sem, xnt_ready.now(b, n))
                    for m in range(DC):
                        for k in range(DC):
                            ins = pe.matmul(T[1][:, m * P:(m + 1) * P], wq[:, k, m * P:(m + 1) * P], XNT[:, k, :], start=(k == 0), stop=(k == DC - 1))
                    ins.then_inc(q_done.sem, 1)

                def scores(g):
                    ch, h = g % UT // 2, g % 2 * HU
                    for k in range(2):
                        ins = pe.matmul(SC[g % 2][:, k, 0:2 * NCTX], QT[:, g // UT % 2, ch, :],
                                        KB[:, ch, h + 2 * k:h + 2 * k + 2, :].rearrange("p h n -> p (h n)"), start=True, stop=True)
                    ins.then_inc(scored.sem, 1)

                turn_xn(0, 0)
                queries(0, 0)
                with pe.Fori(0, BATCH) as b:
                    def at(q, n):
                        if n < 0:
                            pe.wait_ge(q.sem, q.prev(b, q.per + n))
                        else:
                            pe.wait_ge(q.sem, q.now(b, n))

                    def times_v(g):
                        at(main_kept, g)
                        at(tail_kept, g)
                        at(o_ready, g - 2)
                        for h in range(HU):
                            head = g % UT * HU + h
                            pe.matmul(OB[g % 2][:, h * VW:(h + 1) * VW], EM[:, g % 2, h, :], VM[:, head * V1W:head * V1W + VW],
                                      start=(h == 0), stop=False, skip_group_check=True)
                        out = OB[g % 2][:, 0:HU * VW].rearrange("p (h w) -> p h w", w=VW)[:, :, 0:V1W]
                        pe.matmul(out, EL[:, g % 2, :], VT[:, g % UT * (HU * V1W):(g % UT + 1) * (HU * V1W)].rearrange("p (h w) -> p h w", w=V1W),
                                  start=False, stop=True, skip_group_check=True).then_inc(av_done.sem, 1)

                    def turn_o(n):
                        at(o_ready, n * UT + UT - 1)
                        for k in range(DC):
                            ins = pe.transpose(T[0][:, k * P:(k + 1) * P], O[:, n % 2, k * P:(k + 1) * P], ident[:])
                        ins.then_inc(o_turned.sem, 1)

                    def project(n):
                        at(ot_ready, n)
                        for k in range(DC):
                            ins = pe.matmul(T[1][:, 0:D], OT[:, k, :], wo[:, k, :], start=(k == 0), stop=(k == DC - 1))
                        ins.then_inc(y_done.sem, 1)

                    at(kb_ready, 0)
                    at(qt_ready, 0)
                    scores(0)
                    for g in range(U):
                        n, u = g // UT, g % UT
                        if u == 0:
                            if n:
                                at(main_kept, g - 1)
                            turn_xn(b, n + 1)
                        if u == 1:
                            at(tail_kept, g - 1)
                            queries(b, n + 1)
                            if n:
                                at(main_kept, g - 1)
                                turn_o(n - 1)
                        if u == 2 and n:
                            at(tail_kept, g - 1)
                            project(n - 1)
                        if g + 1 < U:
                            if u == UT - 1:
                                at(qt_ready, n + 1)
                            scores(g + 1)
                        at(exp_done, g)
                        if u == 0:
                            at(xnt_ready, n + 1)
                        elif u == 1 and n:
                            at(ot_ready, n - 1)
                        else:
                            at(main_kept, g - 1)
                        for h in range(HU):
                            ins = pe.transpose(T[0][:, h * P:(h + 1) * P], E[:, g % 2, h, :], ident[:])
                        ins.then_inc(main_turned.sem, 1)
                        if g == 0:
                            at(x3_ready, -1)
                        elif u == 1:
                            at(qt_ready, n + 1)
                        elif u == 2 and n:
                            at(x3_ready, n - 1)
                        else:
                            at(tail_kept, g - 1)
                        pe.transpose(T[1][:, 0:P], EP[:, g % 2, :, :].rearrange("p h n -> p (h n)"), ident[:]).then_inc(tail_turned.sem, 1)
                        if g == 1:
                            at(v_loaded, 1)
                        if g:
                            times_v(g - 1)
                    times_v(U - 1)
                    turn_o(N - 1)
                    project(N - 1)

            @block.scalar
            def _(a):
                for q in (xnt_ready, exp_done, main_kept, tail_kept, ot_ready):
                    q.start(a)

                def xnt_out(b, n):
                    a.wait_ge(xn_turned.sem, xn_turned.now(b, n))
                    a.copy(XNT[:].rearrange("p a b -> p (a b)"), T[0][:, 0:D]).then_inc(xnt_ready.sem, 1)

                a.wait_ge(setup, 4)
                xnt_out(0, 0)
                with a.Fori(0, BATCH) as b:
                    def exp(g):
                        a.wait_ge(lowered.sem, lowered.now(b, g))
                        a.activation(EP[:, g % 2, :, 0:TAIL], SB[:, g % 2, :, P:NCTX], ACT.Exp)
                        a.activation(E[:, g % 2, :, :], SB[:, g % 2, :, 0:P], ACT.Exp).then_inc(exp_done.sem, 1)

                    def ot_out(n):
                        a.wait_ge(o_turned.sem, o_turned.now(b, n))
                        a.copy(OT[:].rearrange("p a b -> p (a b)"), T[0][:, 0:D]).then_inc(ot_ready.sem, 1)

                    exp(0)
                    for g in range(U):
                        n, u = g // UT, g % UT
                        if u == 0:
                            xnt_out(b, n + 1)
                        if u == 1 and n:
                            ot_out(n - 1)
                        a.wait_ge(main_turned.sem, main_turned.now(b, g))
                        a.copy(EM[:, g % 2, :, :].rearrange("p a b -> p (a b)"), T[0][:]).then_inc(main_kept.sem, 1)
                        a.wait_ge(tail_turned.sem, tail_turned.now(b, g))
                        a.copy(EL[:, g % 2, :], T[1][:, 0:P]).then_inc(tail_kept.sem, 1)
                        if g + 1 < U:
                            exp(g + 1)
                    ot_out(N - 1)

            @block.vector
            def _(v):
                for q in (ix_ready, kb_ready, x2_ready, stats, xn_ready, qt_ready, lowered, o_ready, x3_ready):
                    q.start(v)

                def row_numbers(tile, s):
                    v.tensor_scalar(IX[:, s:s + 1], POS[:, tile], 1.0, None, ALU.mult).then_inc(ix_ready.sem, 1)

                for s in range(4):
                    row_numbers(slice(s, s + 1), s)
                v.memset(VM[:], 0.0).then_inc(setup, 1)
                v.memset(EP[:], 0.0).then_inc(setup, 1)
                v.wait_ge(consts, 16 * NCONST)

                def sum_stats(b, n, mark, last):
                    s = n % 4
                    v.wait_ge(x_loaded[s].sem, x_loaded[s].now(b, n // 4))
                    v.wait_ge(g_loaded[s].sem, g_loaded[s].now(b, n // 4))
                    v.tensor_tensor(X2[:, s, :], XA[:, s, :], G[:, s, :], ALU.add).then_inc(x2_ready.sem, 1)
                    v.wait_ge(x2_ready.sem, x2_ready.now(b, n))
                    v.bn_stats(st[:, s, :], X2[:, s, :]).then_inc(*mark())
                    v.tensor_tensor(XB[:, s, :], X2[:, s, :], bo[:], ALU.add)
                    v.wait_ge(*last())
                    v.memset(fence[:], 0.0)
                    v.bn_aggr(mv[:, s, :], st[:, s, :]).then_inc(stats.sem, 1)

                def norm(b, n):
                    s = n % 4
                    v.wait_ge(rstd.sem, rstd.now(b, n))
                    v.tensor_scalar(XN[:, n % 2, :], X2[:, s, :], mv[:, s, 0:1], rs[:, s, 1:2], ALU.subtract, ALU.mult).then_inc(xn_ready.sem, 1)

                def qt_out(b, n):
                    v.wait_ge(q_done.sem, q_done.now(b, n))
                    for k in range(DC):
                        ins = v.tensor_scalar(QT[:, n % 2, k, :], T[1][:, k * P:(k + 1) * P], bq[:, k:k + 1], scale, ALU.add, ALU.mult)
                    ins.then_inc(qt_ready.sem, 1)

                for n in range(2):
                    sum_stats(0, n, lambda: (dve0, 1), lambda n=n: (dve0, n + 1))
                    row_numbers(slice(n + 4, n + 5), n)
                    norm(0, n)
                qt_out(0, 0)
                with v.Fori(0, BATCH) as b:
                    def lower(g):
                        s4 = SC[g % 2][:, :, 0:2 * NCTX].rearrange("p k (h n) -> p k h n", n=NCTX)
                        v.wait_ge(scored.sem, scored.now(b, g))
                        v.tensor_reduce(mx[:, g % 2, :], s4, AX_X, ALU.max).then_inc(*dve.mark())
                        v.wait_ge(dve.sem, dve.last(b))
                        v.tensor_tensor(SB[:, g % 2, :, :].rearrange("p (k h) n -> p k h n", k=2), s4,
                                        mx[:, g % 2, :].rearrange("p (k h) -> p k h", k=2).unsqueeze(3).to_broadcast([P, 2, 2, NCTX]),
                                        ALU.subtract).then_inc(lowered.sem, 1)

                    def o_out(g):
                        o3 = OB[g % 2][:, 0:HU * VW].rearrange("p (h w) -> p h w", w=VW)
                        v.wait_ge(av_done.sem, av_done.now(b, g))
                        v.reciprocal(rden[:, g % 2, :, :], o3[:, :, HD1:V1W]).then_inc(*dve.mark())
                        v.wait_ge(dve.sem, dve.last(b))
                        v.tensor_tensor(O[:, g // UT % 2, :].rearrange("p (h d) -> p h d", d=HD1)[:, g % UT * HU:(g % UT + 1) * HU, :], o3[:, :, 0:HD1],
                                        rden[:, g % 2, :, :].to_broadcast([P, HU, HD1]), ALU.mult).then_inc(o_ready.sem, 1)

                    def x3_out(n):
                        s = n % 4
                        v.wait_ge(y_done.sem, y_done.now(b, n))
                        v.wait_ge(stored[s].sem, stored[s].now(b, n // 4 - 1))
                        v.tensor_tensor(X3[:, s, :], T[1][:, 0:D], XB[:, s, :], ALU.add).then_inc(x3_ready.sem, 1)

                    v.wait_ge(k_loaded.sem, k_loaded.now(b, 0))
                    for k in range(DC):
                        for h in range(P // HD1):
                            ins = v.tensor_scalar(KB[:, k, h, :], K1[:, k, :], own[:, h:h + 1], None, ALU.mult)
                    ins.then_inc(kb_ready.sem, 1)
                    lower(0)
                    for g in range(U):
                        n, u = g // UT, g % UT
                        if u == 1:
                            qt_out(b, n + 1)
                        if u == 2 and n:
                            x3_out(n - 1)
                        if g + 1 < U:
                            lower(g + 1)
                        if g:
                            o_out(g - 1)
                        if u == 1:
                            sum_stats(b, n + 2, dve.mark, lambda: (dve.sem, dve.last(b)))
                            row_numbers(bass.ds(b * N + n + 6, 1), (n + 2) % 4)
                        if u == 2:
                            norm(b, n + 2)
                    o_out(U - 1)
                    x3_out(N - 1)
                    dve.done()
    sems.release()


def local_layers(nc, c, w, scratch, out):
    N = TPB
    INNER = HL * HDL
    UH = HL // 2
    U = 2 * N
    IC = INNER // P
    GW = S * P
    NG = N // S
    sems = Semaphores(nc)
    with ExitStack() as es:
        def sb(name, shape, dt=F32):
            return es.enter_context(nc.sbuf_tensor("s6_" + name, shape, dt))

        def sem(name):
            return sems.take("s6_" + name)

        def sig(name, per, unit=1, ahead=1):
            return Signal(sem(name), per, unit, ahead)

        def psum(name, banks):
            return es.enter_context(nc.psum_tensor("s6_" + name, [P, banks * 512], F32))

        ident = c["ident"]
        wqkv = sb("wqkv", [P, DC, 3 * INNER])
        wo = sb("wo", [P, IC, D])
        gains = sb("gains", [P, 4, HDL])
        w1 = sb("w1", [P, DC, 2 * HC, HCW])
        w2 = sb("w2", [HCW, HC, D])
        b1 = sb("b1", [HCW, 2 * HC])
        b2 = sb("b2", [P, D])
        ln = sb("ln", [P, 2 * DC])
        turns = sb("turns", [P, N, 4, HDL])
        mask = sb("mask", [P, 2, 2 * P])
        mean_of = sb("mean_of", [P, P])
        mhalf = sb("mhalf", [P, 2 * HL])
        eps = sb("eps", [P, N])
        fence = sb("fence", [P, 1])
        XR = sb("XR", [P, N, D])
        XS = sb("XS", [P, N, D])
        X = sb("X", [P, N, D])
        XTA = sb("XTA", [P, DC, SEQ + 1])
        XTB = sb("XTB", [P, DC, SEQ + 1])
        st = sb("st", [P, N, 6])
        mv = sb("mv", [P, N, 2])
        rs = sb("rs", [P, 2, N])
        RT = sb("RT", [P, N, 4, HDL])
        M1 = sb("M1", [P, 2, INNER])
        M2 = sb("M2", [P, 2, INNER])
        RQ = sb("RQ", [P, 2, INNER])
        SQ = sb("SQ", [P, 2, INNER])
        ss = sb("ss", [P, 2 * HL])
        ssm = sb("ssm", [P, 2 * HL])
        rn = sb("rn", [P, 2 * HL, 1])
        QZ = sb("QZ", [P, HL, P])
        KT = sb("KT", [P, IC, N + 1, P])
        V = sb("V", [P, N + 1, INNER])
        SBE = sb("SBE", [P, 2, 2, UH, 2 * P])
        SM, E = SBE[:, 0], SBE[:, 1]
        nm = sb("nm", [P, U, UH])
        den = sb("den", [P, U, UH])
        rden = sb("rden", [P, U, UH])
        ET = sb("ET", [P, 2, 2, UH, P])
        O = sb("O", [P, INNER])
        OT = sb("OT", [P, IC, P])
        HM = M1
        HN = (M2, RQ)
        GE = sb("GE", [HCW, 2, GW])
        UT = SBE[0:HCW].rearrange("p a b h n -> p (a b h n)")[:, 0:HC * GW].rearrange("p (c n) -> p c n", n=GW)
        rv = sb("rv", [P, 2, GW])
        QK = psum("QK", 2)
        SC = psum("SC", 2)
        VB = psum("VB", 1)
        T = [psum(f"T{k}", 1) for k in range(2)]
        OB = psum("OB", 1)
        MEAN, VAR = (QK[:, 0:512], OB[:]), (QK[:, 512:1024], OB[:])

        consts = sem("consts")
        setup = sem("setup")
        xr_loaded = sig("xr_loaded", 1, 16)
        xs_loaded = sig("xs_loaded", 1, 16)
        a_loaded = sig("a_loaded", 3, 16)
        b_loaded = sig("b_loaded", 5, 16)
        stats = sig("stats", 1)
        rs_ready = sig("rs_ready", 1)
        xa_ready = sig("xa_ready", 4)
        xa_turned = sig("xa_turned", 12)
        xta_ready = sig("xta_ready", 12)
        qk_done = sig("qk_done", N)
        sq_done = sig("sq_done", N)
        qk_read = sig("qk_read", N)
        ss_ready = sig("ss_ready", N)
        rn_ready = sig("rn_ready", N)
        rq_ready = sig("rq_ready", N)
        v_done = sig("v_done", N)
        v_kept = sig("v_kept", N)
        q_turned = sig("q_turned", N)
        k_turned = sig("k_turned", N)
        qz_ready = sig("qz_ready", N)
        kt_ready = sig("kt_ready", N)
        scored = sig("scored", U)
        masked = sig("masked", U)
        nm_ready = sig("nm_ready", U)
        exp_done = sig("exp_done", U)
        ep_turned = sig("ep_turned", U)
        eo_turned = sig("eo_turned", U)
        ep_kept = sig("ep_kept", U)
        eo_kept = sig("eo_kept", U)
        av_done = sig("av_done", U)
        o_ready = sig("o_ready", U)
        o_turned = sig("o_turned", N)
        ot_ready = sig("ot_ready", N)
        y_done = sig("y_done", N)
        x1_ready = sig("x1_ready", N)
        x1_turned = sig("x1_turned", N)
        xtb_ready = sig("xtb_ready", N)
        mean_done = sig("mean_done", NG)
        hm_ready = sig("hm_ready", NG)
        hsq_done = sig("hsq_done", NG)
        var_done = sig("var_done", NG)
        rv_ready = sig("rv_ready", NG)
        hn_ready = sig("hn_ready", NG)
        g_done = sig("g_done", NG * HC)
        a_done = sig("a_done", NG * HC)
        ge_ready = sig("ge_ready", NG * HC)
        u_ready = sig("u_ready", NG * HC)
        w2_done = sig("w2_done", N)
        x2_ready = sig("x2_ready", N // 2)
        final = sig("final", 1)
        stored = sig("stored", 1, 16)
        NCONST = 2
        dve = Steps(sem("dve_steps"), 2 * N + U + 1 + 3 * NG)
        statted = sem("statted")
        pool_sum = sem("pool_sum")

        with nc.Block() as block:
            @block.sync
            def _(sp):
                for q in (xr_loaded, xs_loaded, a_loaded, b_loaded, stored):
                    q.start(sp)

                def load_a(layer):
                    for dst, src in ((wqkv, w["wqkv"]), (wo, w["wo"])):
                        sp.dma_start(dst[:], src[bass.ds(layer, 1)].rearrange("l p a b -> (l p) a b")).then_inc(a_loaded.sem, 16)
                    sp.dma_start(gains[:], w["lgains"][bass.ds(layer, 1)].rearrange("l a b -> (l a) b").partition_broadcast(P)).then_inc(a_loaded.sem, 16)

                def load_b(layer):
                    sp.dma_start(w1[:], w["w1"][bass.ds(layer, 1)].rearrange("l p a b c -> (l p) a b c")).then_inc(b_loaded.sem, 16)
                    sp.dma_start(w2[:], w["w2"][bass.ds(layer, 1)].rearrange("l p a b -> (l p) a b")).then_inc(b_loaded.sem, 16)
                    for dst, src in ((b1, w["lb1"]), (ln, w["lln"])):
                        sp.dma_start(dst[:], src[bass.ds(layer, 1)].rearrange("l p a -> (l p) a")).then_inc(b_loaded.sem, 16)
                    sp.dma_start(b2[:], w["lb2"][bass.ds(layer, 1)].rearrange("l a -> (l a)").partition_broadcast(P)).then_inc(b_loaded.sem, 16)

                def load_x(dst, b, loaded):
                    sp.dma_start(dst[:], scratch["x3"][bass.ds(b * SEQ, SEQ), :].rearrange("(n p) d -> p n d", p=P)).then_inc(loaded.sem, 16)

                load_x(XS, 0, xs_loaded)
                sp.wait_ge(xs_loaded.sem, xs_loaded.now(0, 0))
                load_a(0)
                sp.dma_start(turns[:], w["turns"]).then_inc(consts, 16)
                sp.dma_start(mask[:], w["lmask"]).then_inc(consts, 16)
                load_b(0)
                with sp.Fori(0, BATCH) as b:
                    sp.wait_ge(stored.sem, stored.prev(b, 0))
                    load_x(XR, b, xr_loaded)
                    sp.wait_ge(xa_ready.sem, xa_ready.now(b, 3))
                    load_x(XS, (b + 1) % BATCH, xs_loaded)
                    with sp.Fori(0, DEPTH) as l:
                        i = b * DEPTH + l
                        sp.wait_ge(y_done.sem, y_done.now(i, N - 1))
                        load_a((l + 1) % DEPTH)
                        sp.wait_ge(w2_done.sem, w2_done.now(i, N - 1))
                        load_b((l + 1) % DEPTH)
                    sp.wait_ge(final.sem, final.now(b, 0))
                    sp.dma_start(out[bass.ds(b * SEQ, SEQ), :].rearrange("(n p) d -> p n d", p=P), XR[:]).then_inc(stored.sem, 16)
                sp.wait_ge(stored.sem, stored.now(BATCH - 1, 0))
                sp.wait_ge(xs_loaded.sem, xs_loaded.now(BATCH, 0))
                sp.wait_ge(a_loaded.sem, a_loaded.now(BATCH * DEPTH, 2))
                sp.wait_ge(b_loaded.sem, b_loaded.now(BATCH * DEPTH, 4))

            @block.gpsimd
            def _(gp):
                for q in (rs_ready, rn_ready):
                    q.start(gp)
                gp.memset(mhalf[:], -0.5).then_inc(setup, 1)
                gp.memset(eps[:], EPS).then_inc(setup, 1)
                gp.wait_ge(setup, 8)
                def inverse_deviations(k):
                    gp.wait_ge(stats.sem, stats.now(k, 0))
                    gp.tensor_tensor(rs[:, 0, :], mv[:, :, 1], eps[:], ALU.add).then_inc(pool_sum, 1)
                    gp.wait_ge(pool_sum, k + 1)
                    gp.tensor_tensor(rs[:, 1, :], rs[:, 0, :], mhalf[:, 0:N], ALU.pow).then_inc(rs_ready.sem, 1)

                inverse_deviations(0)
                with gp.Fori(0, BATCH * DEPTH) as i:
                    for n in range(N):
                        gp.wait_ge(ss_ready.sem, ss_ready.now(i, n))
                        gp.tensor_tensor(rn[:].rearrange("p h a -> p (h a)"), ssm[:], mhalf[:], ALU.pow).then_inc(rn_ready.sem, 1)
                    inverse_deviations(i + 1)

            @block.tensor
            def _(pe):
                for q in (xa_turned, qk_done, v_done, q_turned, k_turned, scored, ep_turned, eo_turned, av_done, o_turned,
                          y_done, x1_turned, mean_done, var_done, g_done, a_done, w2_done):
                    q.start(pe)
                pe.wait_ge(setup, 8)

                def turn_pair(b, j, first_tile):
                    for k in range(DC):
                        for t in range(2):
                            ins = pe.transpose(VB[:, (2 * k + t) * P:(2 * k + t + 1) * P], X[:, first_tile + t, k * P:(k + 1) * P], ident[:])
                    ins.then_inc(xa_turned.sem, 1)

                with pe.Fori(0, BATCH) as b:
                    for j in range(4):
                        pe.wait_ge(xa_ready.sem, xa_ready.now(b, j))
                        if j:
                            pe.wait_ge(xta_ready.sem, xta_ready.now(b, j - 1))
                        else:
                            pe.wait_ge(xta_ready.sem, xta_ready.prev(b, 11))
                        turn_pair(b, j, 2 * j)
                    with pe.Fori(0, DEPTH) as l:
                        i = b * DEPTH + l

                        def at(q, n):
                            pe.wait_ge(q.sem, q.now(i, n))

                        def query_key(n, m):
                            if n and m == 0:
                                at(qk_read, n - 1)
                            for k in range(DC):
                                ins = pe.matmul(QK[:, m * 512:(m + 1) * 512], XTA[:, k, n * P:(n + 1) * P], wqkv[:, k, m * INNER:(m + 1) * INNER],
                                                start=(k == 0), stop=(k == DC - 1))
                            if m:
                                ins.then_inc(qk_done.sem, 1)

                        def values(n):
                            if n > 2:
                                at(xtb_ready, n - 3)
                            elif n:
                                at(v_kept, n - 1)
                            for k in range(DC):
                                ins = pe.matmul(VB[:], XTA[:, k, n * P:(n + 1) * P], wqkv[:, k, 2 * INNER:3 * INNER], start=(k == 0), stop=(k == DC - 1))
                            ins.then_inc(v_done.sem, 1)

                        def turn_qk(n):
                            at(rq_ready, n)
                            for m, q in enumerate((q_turned, k_turned)):
                                if n > 1 and m == 0:
                                    at(x1_ready, n - 2)
                                elif n:
                                    at((ep_kept, eo_kept)[m], 2 * n - 2)
                                for k in range(IC):
                                    ins = pe.transpose(T[m][:, k * P:(k + 1) * P], RQ[:, m, k * P:(k + 1) * P], ident[:])
                                ins.then_inc(q.sem, 1)

                        def scores(g):
                            n, u = g // 2, g % 2
                            if u == 0:
                                at(qz_ready, n)
                                at(kt_ready, n)
                            if g:
                                at(masked, g - 1)
                            for h in range(UH):
                                head = u * UH + h
                                ins = pe.matmul(SC[:, h * 2 * P:(h + 1) * 2 * P], QZ[:, head, :], KT[:, head // 2, n:n + 2, :].rearrange("p a n -> p (a n)"),
                                                start=True, stop=True)
                            ins.then_inc(scored.sem, 1)

                        def turn_e(g):
                            n, u = g // 2, g % 2
                            at(exp_done, g)
                            for m, (kept, done) in enumerate(((ep_kept, ep_turned), (eo_kept, eo_turned))):
                                if u and n + 1 < N:
                                    at((qz_ready, kt_ready)[m], n + 1)
                                elif u and m == 0:
                                    at(x1_ready, n - 1)
                                elif g:
                                    at(kept, g - 1)
                                for h in range(UH):
                                    ins = pe.transpose(T[m][:, h * P:(h + 1) * P], E[:, g % 2, h, m * P:(m + 1) * P], ident[:])
                                ins.then_inc(done.sem, 1)

                        def times_v(g):
                            n, u = g // 2, g % 2
                            at(ep_kept, g)
                            at(eo_kept, g)
                            if u == 0:
                                at(v_kept, n)
                            if g:
                                at(o_ready, g - 1)
                            for h in range(UH):
                                pair = (u * UH + h) // 2
                                for m in range(2):
                                    ins = pe.matmul(OB[:, h * P:(h + 1) * P], ET[:, g % 2, m, h, :], V[:, n + m, pair * P:(pair + 1) * P],
                                                    start=(m == 0), stop=(m == 1))
                            ins.then_inc(av_done.sem, 1)

                        def turn_o(n):
                            at(o_ready, 2 * n + 1)
                            at(ep_kept, min(2 * n + 2, U - 1))
                            for k in range(IC):
                                ins = pe.transpose(T[0][:, k * P:(k + 1) * P], O[:, k * P:(k + 1) * P], ident[:])
                            ins.then_inc(o_turned.sem, 1)

                        def project(n):
                            at(ot_ready, n)
                            for k in range(IC):
                                ins = pe.matmul(T[0][:, 0:D], OT[:, k, :], wo[:, k, :], start=(k == 0), stop=(k == IC - 1))
                            ins.then_inc(y_done.sem, 1)

                        def turn_x(n):
                            at(x1_ready, n)
                            if n + 2 < N:
                                at(v_kept, n + 2)
                            else:
                                at(xtb_ready, n - 1)
                            for k in range(DC):
                                ins = pe.transpose(VB[:, k * P:(k + 1) * P], X[:, n, k * P:(k + 1) * P], ident[:])
                            ins.then_inc(x1_turned.sem, 1)

                        def sums(q, src, ready, done, dst):
                            at(*ready)
                            for k in range(DC):
                                ins = pe.matmul(dst, mean_of[:], src(k), start=(k == 0), stop=(k == DC - 1))
                            ins.then_inc(done.sem, 1)

                        def mean(q):
                            at(qk_read, N - 1) if q == 0 else at(o_ready, U - 1)
                            sums(q, lambda k: XTB[:, k, q * GW:(q + 1) * GW], (xtb_ready, (q + 1) * S - 1), mean_done, MEAN[q])

                        def variance(q):
                            sums(q, lambda k: SQ[:, k, :], (hsq_done, q), var_done, VAR[q])

                        def gate_value(q, ch):
                            a = (QK, SC)[ch % 2]
                            j = q * HC + ch
                            if ch == 0:
                                at(hn_ready, q)
                            if j > 1:
                                at(u_ready, j - 2)
                            elif j:
                                at(masked, U - 1)
                            for m, done in ((0, g_done), (1, a_done)):
                                for k in range(DC):
                                    ins = pe.matmul(a[0:HCW, m * 512:m * 512 + GW], w1[:, k, (1 - m) * HC + ch, :], HN[q % 2][:, k, :],
                                                    start=(k == 0), stop=(k == DC - 1))
                                ins.then_inc(done.sem, 1)

                        def down(q, s):
                            if q and s % 2 == 0:
                                at(x2_ready, 2 * q - 2 + s // 2)
                            for ch in range(HC):
                                if s == 0:
                                    at(u_ready, q * HC + ch)
                                ins = pe.matmul(T[s // 2][:, s % 2 * D:(s % 2 + 1) * D], UT[:, ch, s * P:(s + 1) * P], w2[:, ch, :],
                                                start=(ch == 0), stop=(ch == HC - 1))
                            ins.then_inc(w2_done.sem, 1)

                        def turn_x2(j):
                            at(x2_ready, j)
                            if j:
                                pe.wait_ge(xta_ready.sem, xta_ready.now(b, 4 * l + 4 + j - 1))
                            turn_pair(b, j, 2 * j)

                        at(a_loaded, 2)
                        pe.wait_ge(xta_ready.sem, xta_ready.now(b, 4 * l))
                        query_key(0, 0)
                        query_key(0, 1)
                        pe.wait_ge(xta_ready.sem, xta_ready.now(b, 4 * l + 3))
                        values(0)
                        turn_qk(0)
                        query_key(1, 0)
                        scores(0)
                        query_key(1, 1)
                        for n in range(N):
                            scores(2 * n + 1)
                            if n:
                                times_v(2 * n - 1)
                            turn_e(2 * n)
                            if n:
                                turn_o(n - 1)
                            if n + 1 < N:
                                values(n + 1)
                            else:
                                mean(0)
                            times_v(2 * n)
                            if n:
                                project(n - 1)
                            if n + 1 < N:
                                turn_qk(n + 1)
                                if n + 2 < N:
                                    query_key(n + 2, 0)
                                scores(2 * n + 2)
                                if n + 2 < N:
                                    query_key(n + 2, 1)
                            turn_e(2 * n + 1)
                            if n == N - 1:
                                variance(0)
                            if n:
                                turn_x(n - 1)
                        times_v(U - 1)
                        turn_o(N - 1)
                        project(N - 1)
                        at(b_loaded, 4)
                        gate_value(0, 0)
                        turn_x(N - 1)
                        gate_value(0, 1)

                        for q in range(NG):
                            for ch in range(HC):
                                if (q, ch) not in ((0, 0), (0, 1)):
                                    gate_value(q, ch)
                                if ch == 1 and q + 1 < NG:
                                    mean(q + 1)
                                if ch == 3 and q + 1 < NG:
                                    variance(q + 1)
                                if ch in (1, 3) and q:
                                    turn_x2(2 * q - 2 + ch // 2)
                            for s in range(S):
                                down(q, s)
                                if q == NG - 1 and s == 2:
                                    turn_x2(2 * NG - 2)
                        turn_x2(2 * NG - 1)

            @block.scalar
            def _(a):
                for q in (xta_ready, sq_done, v_kept, qz_ready, kt_ready, exp_done, ep_kept, eo_kept, ot_ready, xtb_ready, hsq_done, rv_ready, ge_ready):
                    q.start(a)
                a.wait_ge(setup, 8)

                def keep_turned(dst, tiles, first_tile, ready):
                    w = tiles * P
                    a.copy(dst[:, 0, first_tile * P:first_tile * P + w], VB[:, 0:w])
                    a.copy(dst[:, 1, first_tile * P + 1:first_tile * P + w + 1], VB[:, w:2 * w]).then_inc(ready, 1)

                with a.Fori(0, BATCH) as b:
                    for j in range(4):
                        a.wait_ge(xa_turned.sem, xa_turned.now(b, j))
                        keep_turned(XTA, 2, 2 * j, xta_ready.sem)
                    with a.Fori(0, DEPTH) as l:
                        i = b * DEPTH + l

                        def at(q, n):
                            a.wait_ge(q.sem, q.now(i, n))

                        def squares(n):
                            at(qk_done, n)
                            if n:
                                at(ss_ready, n - 1)
                            a.activation(SQ[:].rearrange("p m n -> p (m n)"), QK[:], ACT.Square).then_inc(sq_done.sem, 1)

                        def keep_v(n):
                            at(v_done, n)
                            a.copy(V[:, n + 1, :], VB[:]).then_inc(v_kept.sem, 1)

                        def keep_qk(n):
                            at(q_turned, n)
                            for r in range(2):
                                ins = a.copy(QZ[r * HDL:(r + 1) * HDL, r::2, :], T[0][r * HDL:(r + 1) * HDL, :].rearrange("p (a b) -> p a b", b=P))
                            ins.then_inc(qz_ready.sem, 1)
                            at(k_turned, n)
                            a.copy(KT[:, :, n + 1, :], T[1][:].rearrange("p (a b) -> p a b", b=P)).then_inc(kt_ready.sem, 1)

                        def exp(g):
                            at(nm_ready, g)
                            for h in range(UH):
                                ins = a.activation(E[:, g % 2, h, :], SM[:, g % 2, h, :], ACT.Exp, bias=nm[:, g, h:h + 1], accum_out=den[:, g, h:h + 1])
                            ins.then_inc(exp_done.sem, 1)

                        def keep_e(g):
                            for m, (done, kept) in enumerate(((ep_turned, ep_kept), (eo_turned, eo_kept))):
                                at(done, g)
                                a.copy(ET[:, g % 2, m, :, :].rearrange("p a b -> p (a b)"), T[m][:]).then_inc(kept.sem, 1)

                        def keep_o(n):
                            at(o_turned, n)
                            a.copy(OT[:].rearrange("p a b -> p (a b)"), T[0][:]).then_inc(ot_ready.sem, 1)

                        def keep_x(n):
                            at(x1_turned, n)
                            keep_turned(XTB, 1, n, xtb_ready.sem)

                        def hsquares(q):
                            at(hm_ready, q)
                            a.activation(SQ[:], HM[:], ACT.Square).then_inc(hsq_done.sem, 1)

                        def deviation(q):
                            at(var_done, q)
                            a.activation(rv[:, 0, :], VAR[q], ACT.Sqrt, bias=eps[:, 0:1]).then_inc(rv_ready.sem, 1)

                        def keep_x2(j):
                            a.wait_ge(xa_turned.sem, xa_turned.now(b, 4 * l + 4 + j))
                            keep_turned(XTA, 2, 2 * j, xta_ready.sem)

                        squares(0)
                        keep_v(0)
                        keep_qk(0)
                        squares(1)
                        for n in range(N):
                            exp(2 * n)
                            keep_e(2 * n)
                            if n:
                                keep_o(n - 1)
                            if n + 1 < N:
                                keep_v(n + 1)
                                keep_qk(n + 1)
                            exp(2 * n + 1)
                            if n + 2 < N:
                                squares(n + 2)
                            if n + 1 == N:
                                hsquares(0)
                            keep_e(2 * n + 1)
                            if n + 1 == N:
                                deviation(0)
                            if n:
                                keep_x(n - 1)
                        keep_o(N - 1)

                        for q in range(NG):
                            for ch in range(HC):
                                j = q * HC + ch
                                at(g_done, j)
                                a.activation(GE[:, ch % 2, :], (QK, SC)[ch % 2][0:HCW, 0:GW], ACT.Gelu, bias=b1[:, HC + ch:HC + ch + 1]).then_inc(ge_ready.sem, 1)
                                if q == 0 and ch == 1:
                                    keep_x(N - 1)
                                if ch == 2 and q + 1 < NG:
                                    hsquares(q + 1)
                                if ch == 4 and q + 1 < NG:
                                    deviation(q + 1)
                                if ch in (1, 3) and q:
                                    keep_x2(2 * q - 2 + ch // 2)
                        keep_x2(2 * NG - 2)
                        keep_x2(2 * NG - 1)

            @block.vector
            def _(v):
                for q in (stats, xa_ready, qk_read, ss_ready, rq_ready, masked, nm_ready, o_ready, x1_ready,
                          hm_ready, hn_ready, u_ready, x2_ready, final):
                    q.start(v)
                v.memset(QZ[:], 0.0).then_inc(setup, 1)
                v.memset(KT[:, :, 0, :], 0.0).then_inc(setup, 1)
                v.memset(V[:, 0, :], 0.0).then_inc(setup, 1)
                v.memset(mean_of[:], 1.0 / D).then_inc(setup, 1)
                v.memset(XTA[:, :, 0:1], 0.0).then_inc(setup, 1)
                v.memset(XTB[:, :, 0:1], 0.0).then_inc(setup, 1)
                v.wait_ge(setup, 8)
                def x_stats(k):
                    for n in range(N):
                        ins = v.bn_stats(st[:, n, :], XS[:, n, :])
                    ins.then_inc(statted, 1)
                    v.wait_ge(statted, k + 1)
                    v.memset(fence[:], 0.0)
                    for n in range(N):
                        ins = v.bn_aggr(mv[:, n, :], st[:, n, :])
                    ins.then_inc(stats.sem, 1)

                v.wait_ge(xs_loaded.sem, xs_loaded.now(0, 0))
                x_stats(0)
                with v.Fori(0, BATCH) as b:
                    v.wait_ge(final.sem, final.prev(b, 0))
                    v.wait_ge(rs_ready.sem, rs_ready.now(b * DEPTH, 0))
                    for n in range(N):
                        ins = v.tensor_scalar(X[:, n, :], XS[:, n, :], mv[:, n, 0:1], rs[:, 1, n:n + 1], ALU.subtract, ALU.mult)
                        if n % 2:
                            ins.then_inc(xa_ready.sem, 1)
                    with v.Fori(0, DEPTH) as l:
                        i = b * DEPTH + l

                        def at(q, n):
                            v.wait_ge(q.sem, q.now(i, n))

                        def step(ins):
                            ins.then_inc(*dve.mark())
                            v.wait_ge(dve.sem, dve.last(i))

                        heads = lambda t: t.rearrange("p (h d) -> p h d", d=HDL)
                        HH = HDL // 2

                        def sum_squares(n):
                            at(sq_done, n)
                            step(v.tensor_reduce(ss[:], SQ[:].rearrange("p m (h d) -> p (m h) d", d=HDL), AX_X, ALU.add))
                            v.tensor_scalar(ssm[:], ss[:], 1e-24, None, ALU.max).then_inc(ss_ready.sem, 1)

                        def rotate(n, m):
                            src = heads(QK[:, m * 512:(m + 1) * 512])
                            v.tensor_tensor(heads(M1[:, m, :]), src, RT[:, n, 2 * m, :].unsqueeze(1).to_broadcast([P, HL, HDL]), ALU.mult)
                            for r in range(2):
                                ins = v.tensor_tensor(heads(M2[:, m, :])[:, :, r * HH:(r + 1) * HH], src[:, :, (1 - r) * HH:(2 - r) * HH],
                                                      RT[:, n, 2 * m + 1, r * HH:(r + 1) * HH].unsqueeze(1).to_broadcast([P, HL, HH]), ALU.mult)
                            if m:
                                ins.then_inc(qk_read.sem, 1)

                        def norms(n):
                            at(qk_read, n)
                            step(v.tensor_tensor(M1[:], M1[:], M2[:], ALU.add))
                            at(rn_ready, n)
                            if n:
                                at(k_turned, n - 1)
                            v.tensor_tensor(RQ[:].rearrange("p m (h d) -> p (m h) d", d=HDL), M1[:].rearrange("p m (h d) -> p (m h) d", d=HDL),
                                            rn[:].to_broadcast([P, 2 * HL, HDL]), ALU.mult).then_inc(rq_ready.sem, 1)

                        def mask_scores(g):
                            at(scored, g)
                            if g > 1:
                                at(exp_done, g - 2)
                            v.tensor_tensor(SM[:, g % 2, :, :], SC[:].rearrange("p (h n) -> p h n", n=2 * P),
                                            mask[:, min(g // 2, 1), :].unsqueeze(1).to_broadcast([P, UH, 2 * P]), ALU.add).then_inc(masked.sem, 1)

                        def maxima(g):
                            at(masked, g)
                            v.tensor_reduce(nm[:, g, :], SM[:, g % 2, :, :], AX_X, ALU.max, negate=True).then_inc(nm_ready.sem, 1)

                        def head_out(g):
                            at(exp_done, g)
                            step(v.reciprocal(rden[:, g, :], den[:, g, :]))
                            at(av_done, g)
                            if g % 2 == 0 and g:
                                at(o_turned, g // 2 - 1)
                            v.tensor_tensor(O[:, g % 2 * (UH * HDL):(g % 2 + 1) * (UH * HDL)].rearrange("p (a b d) -> p a b d", b=2, d=HDL),
                                            OB[:].rearrange("p (a b d) -> p a b d", b=4, d=HDL)[:, :, 0:4:3, :],
                                            rden[:, g, :].rearrange("p (a b) -> p a b", b=2).unsqueeze(3).to_broadcast([P, UH // 2, 2, HDL]),
                                            ALU.mult).then_inc(o_ready.sem, 1)

                        def x1_out(n):
                            at(y_done, n)
                            v.tensor_tensor(X[:, n, :], T[0][:, 0:D], X[:, n, :], ALU.add).then_inc(x1_ready.sem, 1)

                        v.wait_ge(consts, 16 * NCONST)
                        at(a_loaded, 2)
                        step(v.tensor_tensor(RT[:], turns[:], gains[:].unsqueeze(1).to_broadcast([P, N, 4, HDL]), ALU.mult))
                        def centre(q):
                            at(mean_done, q)
                            v.tensor_tensor(HM[:], XTB[:, :, q * GW:(q + 1) * GW], MEAN[q].unsqueeze(1).to_broadcast([P, DC, GW]),
                                            ALU.subtract).then_inc(hm_ready.sem, 1)

                        def deviations(q):
                            at(rv_ready, q)
                            v.reciprocal(rv[:, 1, :], rv[:, 0, :]).then_inc(*dve.mark())

                        def normalize(q):
                            v.wait_ge(dve.sem, dve.last(i))
                            step(v.tensor_tensor(HN[q % 2][:], HM[:], rv[:, 1, :].unsqueeze(1).to_broadcast([P, DC, GW]), ALU.mult))
                            for k in range(DC):
                                ins = v.tensor_scalar(HN[q % 2][:, k, :], HN[q % 2][:, k, :], ln[:, k:k + 1], ln[:, DC + k:DC + k + 1], ALU.mult, ALU.add)
                            ins.then_inc(hn_ready.sem, 1)

                        def gated(q, ch):
                            j = q * HC + ch
                            at(a_done, j)
                            at(ge_ready, j)
                            v.scalar_tensor_tensor(UT[:, ch, :], (QK, SC)[ch % 2][0:HCW, 512:512 + GW], b1[:, ch:ch + 1], GE[:, ch % 2, :],
                                                   ALU.add, ALU.mult).then_inc(u_ready.sem, 1)

                        def x2_out(q, p):
                            tiles = slice(q * S + 2 * p, q * S + 2 * p + 2)
                            at(w2_done, q * S + 2 * p + 1)
                            v.tensor_tensor(X[:, tiles, :], T[p][:].rearrange("p (a d) -> p a d", d=D), X[:, tiles, :], ALU.add).then_inc(x2_ready.sem, 1)

                        sum_squares(0)
                        rotate(0, 0)
                        rotate(0, 1)
                        norms(0)
                        mask_scores(0)
                        maxima(0)
                        for n in range(N):
                            more = n + 1 < N
                            if more:
                                sum_squares(n + 1)
                            mask_scores(2 * n + 1)
                            if n:
                                head_out(2 * n - 1)
                            if more:
                                rotate(n + 1, 0)
                                rotate(n + 1, 1)
                                norms(n + 1)
                            else:
                                maxima(2 * n + 1)
                                centre(0)
                            head_out(2 * n)
                            if n:
                                x1_out(n - 1)
                            if more:
                                maxima(2 * n + 1)
                            if more:
                                mask_scores(2 * n + 2)
                                maxima(2 * n + 2)
                        head_out(U - 1)
                        at(b_loaded, 4)
                        deviations(0)
                        normalize(0)
                        x1_out(N - 1)

                        for q in range(NG):
                            for ch in range(HC):
                                gated(q, ch)
                                if q == 0 and ch == 2:
                                    at(x1_turned, N - 1)
                                    for k in range(NG):
                                        step(v.tensor_tensor(X[:, k * S:(k + 1) * S, :], X[:, k * S:(k + 1) * S, :],
                                                             b2[:].unsqueeze(1).to_broadcast([P, S, D]), ALU.add))
                                if ch == 1 and q + 1 < NG:
                                    centre(q + 1)
                                if ch == 1 and q == NG - 1:
                                    v.wait_ge(xs_loaded.sem, xs_loaded.now(b + 1, 0))
                                    x_stats(i + 1)
                                if ch == HC - 1 and q + 1 < NG:
                                    deviations(q + 1)
                                    normalize(q + 1)
                            for p in range(2):
                                x2_out(q, p)
                        dve.done()
                    v.wait_ge(x2_ready.sem, x2_ready.now(b * DEPTH + DEPTH - 1, N // 2 - 1))
                    v.wait_ge(xa_turned.sem, xa_turned.now(b, 11))
                    v.wait_ge(xr_loaded.sem, xr_loaded.now(b, 0))
                    v.tensor_tensor(XR[:], X[:], XR[:], ALU.add).then_inc(final.sem, 1)


def _layout(i):
    import numpy as np
    f = {k: np.asarray(v) for k, v in i.items()}
    chunks = lambda m, n: np.ascontiguousarray(m.reshape(n, m.shape[0] // n, -1).transpose(1, 0, 2))
    col = lambda v, n: v.reshape(n, -1).T
    w = {
        "ident": np.eye(P, dtype=np.float32),
        "wl": chunks(np.concatenate([f["L0_xattn_Wq"].T, f["L0_xattn_Wlkv"].T], axis=1), 2),
        "wkv": chunks(f["L0_xattn_Wkv"].T, 2),
        "wk1": chunks(f["L1_xattn_Wk"], 2),
        "wv1": chunks(f["L1_xattn_Wv"], 2),
        "bv1": f["L1_xattn_bv"],
        "cols": np.concatenate([
            col(f["L0_xattn_ln_l_g"], 2), col(f["L0_xattn_ln_l_b"], 2), col(f["L1_xattn_bk"], 2),
            np.tile(f["L0_xattn_qn_g"], 2)[:, None], np.tile(f["L0_xattn_kn_g"], 2)[:, None],
            np.zeros((P, 2), np.float32)], axis=1),
        "wo0": chunks(f["L0_xattn_Wo"].T, 2),
        "bo0": f["L0_xattn_bo"],
        "wr": chunks(np.concatenate([f["L0_ffn_macro_w"], f["L0_ffn_micro_w"].transpose(1, 0, 2).reshape(D, EXPERTS)], axis=1), 2),
        "mask": f["mask_BxS2_bk0"].reshape(1, -1),
        "gx": np.concatenate([col(f["L0_xattn_ln_x_g"], 2), col(f["L0_xattn_ln_x_b"], 2)], axis=1),
    }
    pairs = lambda m: m.reshape(EXPERTS, DC, P, FFN).transpose(2, 0, 1, 3)
    w.update({
        "before": np.triu(np.ones((P, P), np.float32), 1),
        "starts": np.arange(NTS, dtype=np.float32) * P,
        "gate_up": np.stack([pairs(f["L0_ffn_gate_w"]), pairs(f["L0_ffn_up_w"])], axis=3).reshape(P, EXPERTS * DC * 2, FFN),
        "down": f["L0_ffn_down_w"].reshape(EXPERTS, FFN // P, P, D).transpose(2, 0, 1, 3).reshape(P, EXPERTS * FFN // P, D),
        "wq1": chunks(f["L1_xattn_Wq"], DC),
        "wo1": chunks(f["L1_xattn_Wo"], DC),
        "bo1": f["L1_xattn_bo"],
        "cols1": np.concatenate([col(f["L1_xattn_bq"], DC), np.tile(f["L1_xattn_scale"][None], (P, 1)),
                                 np.kron(np.eye(P // HD1, dtype=np.float32), np.ones((HD1, 1), np.float32))], axis=1),
    })
    half = np.arange(0, HDL, 2, dtype=np.float32)
    t = np.arange(SEQ, dtype=np.float32)
    freqs = np.tile(t[:, None] * (1.0 / 10000.0 ** (half / HDL)).astype(np.float32)[None], (1, 2))
    size = ((half + 0.4 * HDL) / (1.4 * HDL))[None] ** ((t - SEQ // 2) / float(P // 2))[:, None]
    size = np.tile(size.astype(np.float32), (1, 2))
    cos, sin = np.cos(freqs), np.sin(freqs) * np.repeat([-1.0, 1.0], HDL // 2)[None]
    turns = np.stack([cos * size * 8, sin * size * 8, cos / size, sin / size], axis=1)
    far, q, k = np.float32(-BIG), np.arange(P)[:, None], np.arange(P)[None]
    before, own = np.where(k >= q, 0, far), np.where(k <= q, 0, far)
    swap = lambda g: np.concatenate([g[:, HDL // 2:], g[:, :HDL // 2]], axis=1)
    gq, gk = f["L1_ffn_q_scale"], f["L1_ffn_k_scale"]
    lchunks = lambda m, n: m.reshape(DEPTH, n, m.shape[1] // n, *m.shape[2:]).swapaxes(1, 2)
    pad = lambda m, axis: np.concatenate([m, np.zeros([HC * HCW - HIDDEN if a == axis else z for a, z in enumerate(m.shape)], np.float32)], axis=axis)
    two = lambda m: pad(m.reshape(*m.shape[:-1], 2, HIDDEN), m.ndim).reshape(*m.shape[:-1], 2 * HC, HCW)
    w.update({
        "turns": turns.reshape(TPB, P, 4, HDL).transpose(1, 0, 2, 3).astype(np.float32),
        "lmask": np.stack([np.concatenate([np.full_like(own, far), own], axis=1), np.concatenate([before, own], axis=1)], axis=1).astype(np.float32),
        "wqkv": lchunks(f["L1_ffn_wqkv"], DC),
        "wo": lchunks(f["L1_ffn_wo"], HL * HDL // P),
        "lgains": np.stack([gq, swap(gq), gk, swap(gk)], axis=1),
        "w1": lchunks(two(f["L1_ffn_w1"]), DC),
        "w2": lchunks(pad(f["L1_ffn_w2"], 1), HC),
        "lb1": two(f["L1_ffn_b1"]).swapaxes(1, 2),
        "lln": np.concatenate([f["L1_ffn_ln_g"].reshape(DEPTH, DC, P).swapaxes(1, 2), f["L1_ffn_ln_b"].reshape(DEPTH, DC, P).swapaxes(1, 2)], axis=2),
        "lb2": f["L1_ffn_b2"],
    })
    return {k: np.ascontiguousarray(v) for k, v in w.items()}


def build(nc, t, y):
    sizes = {
        "q0": (NT, P, 2, P), "k0": (BATCH, P, 2, KEYS0), "v0": (BATCH, P, KC0, D), "k1": (BATCH, P, 2, NCTX), "v1": (BATCH, P, 2, V1),
        "x1": (NTOK, D), "xn": (NTOK, D), "sorted": (NTS * P, XW), "ys": (NTS * P, D), "x3": (NTOK, D),
    }
    scratch = {n: nc.dram_tensor("scratch_" + n, s, F32, kind="Internal").ap() for n, s in sizes.items()}
    with ExitStack() as es:
        def sb(stack, name, shape, dt=F32):
            return stack.enter_context(nc.sbuf_tensor(name, shape, dt))

        c = {"ident": sb(es, "ident", [P, P])}
        with ExitStack() as routing:
            c["rows"] = sb(routing, "rows", [P, NT + TPB])
            c["group"] = sb(routing, "group", [P, NTS], I32)
            c["logits"] = sb(routing, "logits", [P, NT, NR])
            c["weights"] = sb(routing, "weights", [P, NT, 2])
            keys_and_projections(nc, c, t["x"], t["ctx_768"], t, scratch)
            with ExitStack() as moe:
                c["gate_up"] = sb(moe, "gate_up", [P, EXPERTS * DC * 2, FFN])
                sems = Semaphores(nc)
                c["experts_loaded"] = sems.take("experts_loaded")
                attention0(nc, c, t["x"], t, scratch)
                c["down"] = sb(moe, "down", [P, EXPERTS * FFN // P, D])
                route_tokens(nc, c, t, scratch)
                experts(nc, c, t, scratch)
                sems.release()
            attention1(nc, c, t, scratch)
        local_layers(nc, c, t, scratch, y)


def kernel(**inputs):
    import numpy as np
    import concourse.bacc as bacc
    from concourse.bass_utils import run_bass_kernel_spmd as run
    nc = bacc.Bacc("TRN2", target_bir_lowering=False, num_devices=1)
    arrays = _layout(inputs)
    arrays["x"] = np.ascontiguousarray(np.asarray(inputs["x"]).reshape(NTOK, D))
    arrays["ctx_768"] = np.ascontiguousarray(inputs["ctx_768"])
    t = {n: nc.dram_tensor("in_" + n, a.shape, mybir.dt.from_np(a.dtype), kind="ExternalInput").ap() for n, a in arrays.items()}
    y = nc.dram_tensor("y", (NTOK, D), F32, kind="ExternalOutput").ap()
    build(nc, t, y)
    r = run(nc, [{"in_" + n: a for n, a in arrays.items()}], core_ids=[0]).results[0]
    return r["y"].reshape(BATCH, SEQ, D)
```
